# Optimizing a Trainium2 kernel written in Bass

```python
import numpy as np
import jax
import jax.numpy as jnp

def _softmax(x, axis=-1):
    return jax.nn.softmax(x, axis=axis)

def _gelu(x):
    return jax.nn.gelu(x, approximate=True)

def _silu(x):
    return jax.nn.silu(x)

def _sigmoid(x):
    return jax.nn.sigmoid(x)

def _layernorm(x, axis=-1, eps=1e-05):
    m = jnp.mean(x, axis=axis, keepdims=True)
    v = jnp.var(x, axis=axis, keepdims=True)
    return (x - m) / jnp.sqrt(v + eps)

def _scatter_add(tgt, idx, src, axis=0):
    return tgt.at[idx].add(src)

def _segment_sum(src, seg, n):
    return jax.ops.segment_sum(src, seg, n)
kernel_name = 'mk_macaron_d1_jaxref_r8_382a0a'

def setup_inputs(seed: int=0):
    np.random.seed(seed)
    _w = jnp.asarray

    def _L0_attn_setup():
        import jax, jax.numpy as jnp
        import numpy as np
        HEADS = 16
        KV_GROUPS = 4
        SWA_SIZE = 128
        NEG_INF = jnp.float32(-1e+30)
        key = jax.random.key(seed)
        ks = jax.random.split(key, 6)
        B, T, E, M = (1, 512, 256, 256)
        Dkv = M // HEADS * KV_GROUPS
        s = lambda fan: 1.0 / np.sqrt(fan)
        return {'x': jax.random.normal(ks[0], (B, T, E), jnp.float32), 'Wq': jax.random.normal(ks[1], (E, M), jnp.float32) * s(E), 'Wk': jax.random.normal(ks[2], (E, Dkv), jnp.float32) * s(E), 'Wv': jax.random.normal(ks[3], (E, Dkv), jnp.float32) * s(E), 'Wo': jax.random.normal(ks[4], (M, M), jnp.float32) * s(M), 'bo': jnp.zeros((M,), jnp.float32)}
    _L0_attn_in = _L0_attn_setup()

    def _L0_ffn_setup():
        import jax, jax.numpy as jnp
        import numpy as np
        H = 256
        I_MOE = 176
        E = 8
        TOP_K = 2
        NG = 4
        TOPK_G = 2
        SCALE = 2.5
        N_SHARED = 2
        I_SHARED = I_MOE * N_SHARED
        B, S = (1, 256)

        def _mlp(x, gw, uw, dw):
            return jax.nn.silu(x @ gw.T) * (x @ uw.T) @ dw.T

        def _route(x2d, rw, bias):
            T = x2d.shape[0]
            logits = x2d.astype(jnp.float32) @ rw.astype(jnp.float32).T
            scores = jax.nn.sigmoid(logits)
            sfc = scores + bias[None, :]
            grp = sfc.reshape(T, NG, E // NG)
            group_scores = jnp.sum(jax.lax.top_k(grp, 2)[0], axis=-1)
            grp_idx = jax.lax.top_k(group_scores, TOPK_G)[1]
            group_mask = jnp.zeros((T, NG), jnp.float32).at[jnp.arange(T)[:, None], grp_idx].set(1.0)
            score_mask = jnp.repeat(group_mask, E // NG, axis=1)
            masked = jnp.where(score_mask > 0, sfc, 0.0)
            topk_idx = jax.lax.top_k(masked, TOP_K)[1]
            topk_w = jnp.take_along_axis(scores, topk_idx, axis=1)
            topk_w = topk_w / (jnp.sum(topk_w, axis=-1, keepdims=True) + 1e-20)
            return (topk_idx, topk_w * SCALE)
        key = jax.random.key(seed)
        ks = jax.random.split(key, 9)
        sc = 0.02
        return {'x': jax.random.normal(ks[0], (B, S, H), dtype=jnp.float32), 'router_weight': jax.random.normal(ks[1], (E, H), dtype=jnp.float32) * sc, 'e_score_correction_bias': jnp.zeros((E,), dtype=jnp.float32), 'gate_w': jax.random.normal(ks[2], (E, I_MOE, H), dtype=jnp.float32) * sc, 'up_w': jax.random.normal(ks[3], (E, I_MOE, H), dtype=jnp.float32) * sc, 'down_w': jax.random.normal(ks[4], (E, H, I_MOE), dtype=jnp.float32) * sc, 'shared_gate_w': jax.random.normal(ks[5], (I_SHARED, H), dtype=jnp.float32) * sc, 'shared_up_w': jax.random.normal(ks[6], (I_SHARED, H), dtype=jnp.float32) * sc, 'shared_down_w': jax.random.normal(ks[7], (H, I_SHARED), dtype=jnp.float32) * sc}
    _L0_ffn_in = _L0_ffn_setup()
    _d = {'L0_attn_x': _L0_attn_in['x'], 'L0_attn_Wq': _L0_attn_in['Wq'], 'L0_attn_Wk': _L0_attn_in['Wk'], 'L0_attn_Wv': _L0_attn_in['Wv'], 'L0_attn_Wo': _L0_attn_in['Wo'], 'L0_attn_bo': _L0_attn_in['bo'], 'L0_ffn_router_weight': _L0_ffn_in['router_weight'], 'L0_ffn_e_score_correction_bias': _L0_ffn_in['e_score_correction_bias'], 'L0_ffn_gate_w': _L0_ffn_in['gate_w'], 'L0_ffn_up_w': _L0_ffn_in['up_w'], 'L0_ffn_down_w': _L0_ffn_in['down_w'], 'L0_ffn_shared_gate_w': _L0_ffn_in['shared_gate_w'], 'L0_ffn_shared_up_w': _L0_ffn_in['shared_up_w'], 'L0_ffn_shared_down_w': _L0_ffn_in['shared_down_w']}
    _x0 = _d['L0_attn_x']
    _d['L0_attn_x'] = jax.random.normal(jax.random.fold_in(jax.random.key(seed), 1), (1, 1024, 256), dtype=_x0.dtype)
    del _x0
    return _d

def reference(L0_attn_x, L0_attn_Wq, L0_attn_Wk, L0_attn_Wv, L0_attn_Wo, L0_attn_bo, L0_ffn_router_weight, L0_ffn_e_score_correction_bias, L0_ffn_gate_w, L0_ffn_up_w, L0_ffn_down_w, L0_ffn_shared_gate_w, L0_ffn_shared_up_w, L0_ffn_shared_down_w):

    def _L0_attn_ref(x, Wq, Wk, Wv, Wo, bo):
        import jax, jax.numpy as jnp
        import numpy as np
        HEADS = 16
        KV_GROUPS = 4
        SWA_SIZE = 128
        NEG_INF = jnp.float32(-1e+30)
        B, T, E = x.shape
        M = Wq.shape[1]
        D = M // HEADS
        QG = HEADS // KV_GROUPS
        Q = (x @ Wq).reshape(B, T, KV_GROUPS, QG, D)
        K = (x @ Wk).reshape(B, T, KV_GROUPS, D)
        V = (x @ Wv).reshape(B, T, KV_GROUPS, D)
        scores = jnp.einsum('btgqd,bsgd->bgqts', Q, K) / jnp.sqrt(jnp.float32(D))
        i = jnp.arange(T)[:, None]
        j = jnp.arange(T)[None, :]
        allowed = (j <= i) & (i - j < SWA_SIZE)
        scores = jnp.where(allowed[None, None, None], scores, NEG_INF)
        p = jax.nn.softmax(scores, axis=-1)
        att = jnp.einsum('bgqts,bsgd->btgqd', p, V).reshape(B, T, M)
        return att @ Wo + bo

    def _L0_ffn_ref(x, router_weight, e_score_correction_bias, gate_w, up_w, down_w, shared_gate_w, shared_up_w, shared_down_w):
        import jax, jax.numpy as jnp
        import numpy as np
        H = 256
        I_MOE = 176
        E = 8
        TOP_K = 2
        NG = 4
        TOPK_G = 2
        SCALE = 2.5
        N_SHARED = 2
        I_SHARED = I_MOE * N_SHARED
        B, S = (1, 256)

        def _mlp(x, gw, uw, dw):
            return jax.nn.silu(x @ gw.T) * (x @ uw.T) @ dw.T

        def _route(x2d, rw, bias):
            T = x2d.shape[0]
            logits = x2d.astype(jnp.float32) @ rw.astype(jnp.float32).T
            scores = jax.nn.sigmoid(logits)
            sfc = scores + bias[None, :]
            grp = sfc.reshape(T, NG, E // NG)
            group_scores = jnp.sum(jax.lax.top_k(grp, 2)[0], axis=-1)
            grp_idx = jax.lax.top_k(group_scores, TOPK_G)[1]
            group_mask = jnp.zeros((T, NG), jnp.float32).at[jnp.arange(T)[:, None], grp_idx].set(1.0)
            score_mask = jnp.repeat(group_mask, E // NG, axis=1)
            masked = jnp.where(score_mask > 0, sfc, 0.0)
            topk_idx = jax.lax.top_k(masked, TOP_K)[1]
            topk_w = jnp.take_along_axis(scores, topk_idx, axis=1)
            topk_w = topk_w / (jnp.sum(topk_w, axis=-1, keepdims=True) + 1e-20)
            return (topk_idx, topk_w * SCALE)
        orig_shape = x.shape
        x2d = x.reshape(-1, H)
        T = x2d.shape[0]
        topk_idx, topk_w = _route(x2d, router_weight, e_score_correction_bias)
        cw = jnp.zeros((T, E), jnp.float32).at[jnp.arange(T)[:, None], topk_idx].add(topk_w)

        def expert_body(acc, ws):
            gw, uw, dw, cwe = ws
            y = _mlp(x2d, gw, uw, dw)
            return (acc + cwe[:, None] * y, None)
        routed, _ = jax.lax.scan(expert_body, jnp.zeros_like(x2d), (gate_w, up_w, down_w, cw.T))
        out = routed.reshape(orig_shape) + _mlp(x, shared_gate_w, shared_up_w, shared_down_w)
        return out
    x = L0_attn_x
    x = x + 0.5 * _L0_ffn_ref(_layernorm(x, axis=-1), L0_ffn_router_weight, L0_ffn_e_score_correction_bias, L0_ffn_gate_w, L0_ffn_up_w, L0_ffn_down_w, L0_ffn_shared_gate_w, L0_ffn_shared_up_w, L0_ffn_shared_down_w)
    x = x + _L0_attn_ref(_layernorm(x, axis=-1), L0_attn_Wq, L0_attn_Wk, L0_attn_Wv, L0_attn_Wo, L0_attn_bo)
    x = x + 0.5 * _L0_ffn_ref(_layernorm(x, axis=-1), L0_ffn_router_weight, L0_ffn_e_score_correction_bias, L0_ffn_gate_w, L0_ffn_up_w, L0_ffn_down_w, L0_ffn_shared_gate_w, L0_ffn_shared_up_w, L0_ffn_shared_down_w)
    return x

_drawn_inputs = setup_inputs


def setup_inputs(seed=0):
    import zlib

    import numpy as np

    out = dict(_drawn_inputs(seed))
    spreads = {'L0_attn_bo': (0.0, 0.1), 'L0_ffn_e_score_correction_bias': (0.0, 1.496)}
    factors = {'L0_ffn_router_weight': 11.596,
     'L0_ffn_shared_gate_w': 2.938,
     'L0_ffn_shared_up_w': 2.9,
     'L0_ffn_shared_down_w': 2.906,
     'L0_ffn_gate_w': 2.68}
    for name, (base, spread) in spreads.items():
        noise = np.random.default_rng([zlib.crc32(name.encode()), seed]).standard_normal(out[name].shape)
        drawn = base * np.exp(spread * noise) if base else spread * noise
        out[name] = jnp.asarray(drawn.astype(out[name].dtype))
    for name, factor in factors.items():
        out[name] = (out[name] * factor).astype(out[name].dtype)
    return out
```

```python
from contextlib import ExitStack

import concourse.bass as bass
from concourse import mybir

F32 = mybir.dt.float32
F32R = mybir.dt.float32r
BF16 = mybir.dt.bfloat16
I32 = mybir.dt.int32
ALU = mybir.AluOpType
ACT = mybir.ActivationFunctionType
AX_X = mybir.AxisListType.X

P = 128
T = 1024
TT = T // P
H = 256
HC = H // P
E = 8
NG = 4
I_MOE = 176
I_SHARED = 352
SH_BLOCKS = -(-I_SHARED // P)
RT_BLOCKS = E * I_MOE // P
BLOCKS = SH_BLOCKS + RT_BLOCKS
HALF = 512
STEPS = 2 * BLOCKS
GU = 4 * P
WB = GU + H
SCALE = 2.5
EPS = 1e-5

HEADS = 16
KV = 4
QG = HEADS // KV
D = 16
UNITS = TT * KV
QK_SCALE = 0.25
NEG = -1e30
VW = D + 1

C_WQ = 0
C_WK = C_WQ + HC * QG * P
C_WV = C_WK + HC * P
C_WO = C_WV + HC * KV * D
C_RW = C_WO + HC * H
C_END = C_RW + HC * E


def macaron_kernel(nc, x_in, w_blocks, w_small, row_kind, router_bias, out_bias, out):
    with ExitStack() as ctx:
        def sb(name, shape, dt=F32, stack=ctx):
            return stack.enter_context(nc.sbuf_tensor(name, shape, dt))

        def sem(name):
            return ctx.enter_context(nc.semaphore(name))

        bank = [ctx.enter_context(nc.psum_tensor(f"bank{i}", [P, 512], F32)) for i in range(8)]

        x = sb("x", [P, TT, H])
        xh = sb("xh", [P, HC, T], F32R)
        xl = sb("xl", [P, HC, T], F32R)
        wraw = sb("wraw", [P, BLOCKS + 1, WB])
        wh = sb("wh", [P, 2, WB], F32R)
        wl = sb("wl", [P, 2, WB], F32R)
        ah = sb("ah", [P, C_END], F32R)
        al = sb("al", [P, C_END], F32R)
        ident = sb("ident", [P, P])
        zeros = sb("zeros", [P, 512], BF16)
        negs = sb("negs", [P, 2 * P], BF16)
        kinds = sb("kinds", [P, 2])
        rbias = sb("rbias", [P, E])
        obias = sb("obias", [P, H])
        bst = sb("bst", [P, TT, 6])
        mv = sb("mv", [P, TT, 2])
        ve = sb("ve", [P, TT])
        lnv = sb("lnv", [P, TT])
        rs = sb("rs", [P, TT])
        nt = sb("nt", [P, 2, TT])
        r8 = sb("r8", [P, 8, TT * E])
        r4 = sb("r4", [P, 4, TT * NG])
        r16 = sb("r16", [P, 2, TT * NG * NG])
        tie4 = sb("tie4", [P, NG, NG])
        tie8 = sb("tie8", [P, E, E])
        cwt = sb("cwt", [TT * E, P])
        with ExitStack() as ffn_stack:
            cwb = sb("cwb", [P, RT_BLOCKS + 1, T], F32, ffn_stack)
            act_h = sb("act_h", [P, 4, HALF], F32, ffn_stack)
            hh = sb("hh", [P, 4, HALF], F32R, ffn_stack)
            hl = sb("hl", [P, 4, HALF], F32R, ffn_stack)
        with ExitStack() as attn_stack:
            qs = sb("qs", [P, QG, T], F32R, attn_stack)
            qh = sb("qh", [P, 2, HALF], F32R, attn_stack)
            qb = sb("qb", [P, 2, HALF], F32, attn_stack)
            kh = sb("kh", [P, T + P], F32R, attn_stack)
            kl = sb("kl", [P, T + P], F32R, attn_stack)
            qring = sb("qring", [P, 2, QG * P], F32R, attn_stack)
            khring = sb("khring", [P, 2, 2 * P], F32R, attn_stack)
            klring = sb("klring", [P, 2, 2 * P], F32R, attn_stack)
            vx = sb("vx", [P, TT + 1, KV, VW], F32, attn_stack)
            sel_q = sb("sel_q", [P, QG, P], F32, attn_stack)
            cur_k = sb("cur_k", [P, QG, P], F32, attn_stack)
            prev_k = sb("prev_k", [P, QG, P], F32, attn_stack)
            nmax = sb("nmax", [P, 2, QG], F32, attn_stack)
            prob = sb("prob", [P, 2, QG * P], F32, attn_stack)
            pcur = sb("pcur", [P, 2, QG * P], F32, attn_stack)
            pprev = sb("pprev", [P, 2, QG * P], F32, attn_stack)
            idle = sb("idle", [P, 1], F32, attn_stack)
            rden = sb("rden", [P, HEADS], F32, attn_stack)
            att = sb("att", [P, H], F32, attn_stack)
            oh = sb("oh", [P, HC, P], F32R, attn_stack)
            ol = sb("ol", [P, HC, P], F32R, attn_stack)
        wsm = cwb[:, 0:2, :].rearrange("p a b -> p (a b)")
        xn = act_h[:, :, :].rearrange("p a (b n) -> p (a b) n", n=H)
        cw_dram = nc.dram_tensor("cw_dram", (TT * E, P), F32, kind="Internal").ap()

        s_x = sem("s_x")
        s_w = sem("s_w")
        s_small = sem("s_small")
        s_const = sem("s_const")
        s_pool = sem("s_pool")
        s_ah = sem("s_ah")
        s_al = sem("s_al")
        s_dve = sem("s_dve")
        s_ve = sem("s_ve")
        s_ln = sem("s_ln")
        s_rs = sem("s_rs")
        s_xn = sem("s_xn")
        s_xt = sem("s_xt")
        s_xh = sem("s_xh")
        s_xl = sem("s_xl")
        s_logit = sem("s_logit")
        s_er = sem("s_er")
        s_cw = sem("s_cw")
        s_cwt = sem("s_cwt")
        s_cwc = sem("s_cwc")
        s_cwd = sem("s_cwd")
        s_cwb = sem("s_cwb")
        s_ones = sem("s_ones")
        s_guh = sem("s_guh")
        s_gul = sem("s_gul")
        s_dwh = sem("s_dwh")
        s_dwl = sem("s_dwl")
        s_g = sem("s_g")
        s_u = sem("s_u")
        s_silu = sem("s_silu")
        s_cwm = sem("s_cwm")
        s_h = sem("s_h")
        s_hh = sem("s_hh")
        s_hl = sem("s_hl")
        s_down = sem("s_down")
        s_fin = sem("s_fin")
        s_xb = sem("s_xb")
        s_kp = sem("s_kp")
        s_kh = sem("s_kh")
        s_kl = sem("s_kl")
        s_vp = sem("s_vp")
        s_v = sem("s_v")
        s_qp = sem("s_qp")
        s_qh = sem("s_qh")
        s_qb = sem("s_qb")
        s_qs = sem("s_qs")
        s_pads = sem("s_pads")
        s_ring = sem("s_ring")
        s_qk = sem("s_qk")
        s_sel = sem("s_sel")
        s_nm = sem("s_nm")
        s_exp = sem("s_exp")
        s_pt = sem("s_pt")
        s_pm = sem("s_pm")
        s_av = sem("s_av")
        s_rd = sem("s_rd")
        s_att = sem("s_att")
        s_ot = sem("s_ot")
        s_oh = sem("s_oh")
        s_ol = sem("s_ol")
        s_wo = sem("s_wo")
        s_x2 = sem("s_x2")
        s_out = sem("s_out")
        N_PADS = 7
        PAIRS = TT // 2

        block = ctx.enter_context(nc.Block())

        def block_cols(b, a, z):
            if isinstance(b, int):
                return wraw[:, b, a:z]
            return wraw[:, bass.ds(b, 1), a:z].rearrange("p a n -> p (a n)")

        def expert_runs(b):
            at, runs = 0, []
            while at < P:
                e = (b * P + at) // I_MOE
                n = min(P - at, (e + 1) * I_MOE - b * P - at)
                runs.append((at, n, e))
                at += n
            return runs

        N_CWB = sum(len(expert_runs(b)) for b in range(RT_BLOCKS))

        @block.sync
        def _(sp):
            x_tiles = x_in.rearrange("a (t p) h -> p (a t) h", p=P)
            sp.dma_start(x[:, 0:4, :], x_tiles[:, 0:4, :]).then_inc(s_x, 16)
            sp.dma_start(x[:, 4:8, :], x_tiles[:, 4:8, :]).then_inc(s_x, 16)
            sp.dma_start(wsm[:, 0:C_END], w_small).then_inc(s_small, 16)
            sp.dma_start(kinds[:], row_kind).then_inc(s_const, 16)
            sp.dma_start(rbias[:], router_bias.partition_broadcast(P)).then_inc(s_const, 16)
            sp.dma_start(obias[:], out_bias.partition_broadcast(P)).then_inc(s_const, 16)
            wv = w_blocks
            for b in range(0, BLOCKS + 1, 3):
                sp.dma_start(wraw[:, b:b + 3, :], wv[:, b:b + 3, :]).then_inc(s_w, 16)
            for f in range(2):
                sp.wait_ge(s_cwc, f + 1)
                sp.dma_start(cw_dram, cwt[:]).then_inc(s_cwd, 16)
                sp.wait_ge(s_cwd, 16 * (f + 1))
                rows = cw_dram.rearrange("(e t) p -> e (t p)", e=E)
                if f == 0:
                    sp.wait_ge(s_al, 1)
                for b in range(RT_BLOCKS):
                    for at, n, e in expert_runs(b):
                        sp.dma_start(cwb[at:at + n, b + 1, :], rows[e, :].partition_broadcast(n)).then_inc(s_cwb, 16)
            out_tiles = out.rearrange("a (t p) h -> p (a t) h", p=P)
            for b in range(PAIRS):
                sp.wait_ge(s_fin, PAIRS + b + 1)
                sp.dma_start(out_tiles[:, 2 * b:2 * b + 2, :], x[:, 2 * b:2 * b + 2, :]).then_inc(s_out, 16)
            sp.wait_ge(s_out, 16 * PAIRS)

        @block.gpsimd
        def _(pool):
            pool.memset(ident[:], 0.0).then_inc(s_pool, 1)
            pool.memset(zeros[:], 0.0)
            pool.memset(negs[:, 0:P], 1.0 / 32)
            pool.memset(negs[:, P:2 * P], NEG)
            pool.memset(tie4[:], 1.0).then_inc(s_pool, 1)
            pool.memset(tie8[:], 1.0).then_inc(s_pool, 1)
            pool.wait_ge(s_pool, 3)
            pool.affine_select(out=ident[:], in_=ident[:], compare_op=ALU.not_equal, fill=1.0, base=0,
                               pattern=[[-1, P]], channel_multiplier=1).then_inc(s_pool, 1)
            pool.affine_select(out=tie4[:], in_=tie4[:], compare_op=ALU.is_gt, fill=0.0, base=0,
                               pattern=[[1, NG], [-1, NG]], channel_multiplier=0).then_inc(s_pool, 1)
            pool.affine_select(out=tie8[:], in_=tie8[:], compare_op=ALU.is_gt, fill=0.0, base=0,
                               pattern=[[1, E], [-1, E]], channel_multiplier=0).then_inc(s_pool, 1)
            pool.wait_ge(s_ah, 1)
            pool.tensor_tensor(al[:], wsm[:, 0:C_END], ah[:].bitcast(F32), ALU.subtract).then_inc(s_al, 1)
            pool.wait_ge(s_guh, 1)
            pool.tensor_tensor(wl[:, 0, 0:GU], wraw[:, 0, 0:GU], wh[:, 0, 0:GU].bitcast(F32), ALU.subtract).then_inc(s_gul, 1)
            pool.wait_ge(s_dwh, 1)
            pool.tensor_tensor(wl[:, 0, GU:WB], wraw[:, 0, GU:WB], wh[:, 0, GU:WB].bitcast(F32), ALU.subtract).then_inc(s_dwl, 1)
            pool.wait_ge(s_al, 1)
            pool.memset(cwb[:, 0, :], 1.0).then_inc(s_ones, 1)

            def low_parts(f):
                with_base = 1 + BLOCKS * f
                with pool.Fori(0, BLOCKS // 2) as j:
                    for k in range(2):
                        r = (k + 1) % 2
                        pool.wait_ge(s_guh, with_base + 2 * j + k + 1)
                        pool.tensor_tensor(wl[:, r, 0:GU], block_cols(2 * j + k + 1, 0, GU),
                                           wh[:, r, 0:GU].bitcast(F32), ALU.subtract).then_inc(s_gul, 1)
                        pool.wait_ge(s_dwh, with_base + 2 * j + k + 1)
                        pool.tensor_tensor(wl[:, r, GU:WB], block_cols(2 * j + k + 1, GU, WB),
                                           wh[:, r, GU:WB].bitcast(F32), ALU.subtract).then_inc(s_dwl, 1)

            low_parts(0)

            pool.wait_ge(s_down, STEPS)
            pool.wait_ge(s_xl, 2 * PAIRS)
            pool.memset(sel_q[:], 1.0)
            pool.memset(cur_k[:], 1.0)
            pool.memset(prev_k[:], 1.0)
            pool.memset(vx[:, 1:TT + 1, :, D:VW], 1.0)
            pool.memset(vx[:, 0, :, :], 0.0)
            pool.memset(kh[:, 0:P].bitcast(F32), 0.0)
            pool.memset(kl[:, 0:P].bitcast(F32), 0.0).then_inc(s_pads, 1)
            pool.wait_ge(s_pads, 1)
            pool.affine_select(out=sel_q[:], in_=sel_q[:], compare_op=ALU.is_ge, fill=0.0, base=0,
                               pattern=[[0, QG], [-1, P]], channel_multiplier=1)
            pool.affine_select(out=cur_k[:], in_=cur_k[:], compare_op=ALU.is_ge, fill=0.0, base=0,
                               pattern=[[0, QG], [1, P]], channel_multiplier=-1)
            pool.affine_select(out=prev_k[:], in_=prev_k[:], compare_op=ALU.is_gt, fill=0.0, base=0,
                               pattern=[[0, QG], [-1, P]], channel_multiplier=1).then_inc(s_pads, 1)
            pool.wait_ge(s_const, 48)
            for t in range(TT):
                pool.tensor_tensor(x[:, t, :], x[:, t, :], obias[:], ALU.add).then_inc(s_xb, 1)

            def ring(i, k, first):
                if not first:
                    pool.wait_ge(s_qk, 4 * i - 4)
                pool.tensor_copy(qring[:, k, :].rearrange("p (h q) -> p h q", h=QG),
                                 qs[:, :, bass.ds(i * P, P)] if not isinstance(i, int) else qs[:, :, i * P:i * P + P])
                w = bass.ds(i * P, 2 * P) if not isinstance(i, int) else slice(i * P, i * P + 2 * P)
                pool.tensor_copy(khring[:, k, :], kh[:, w])
                pool.tensor_copy(klring[:, k, :], kl[:, w]).then_inc(s_ring, 1)

            pool.wait_ge(s_qs, 2 * QG)
            pool.wait_ge(s_kl, 2)
            ring(0, 0, True)
            ring(1, 1, True)
            with pool.Fori(1, TT // 2) as j:
                for k in range(2):
                    ring(2 * j + k, k, False)
            low_parts(1)

        @block.scalar
        def _(act):
            act.wait_ge(s_small, 16)
            act.activation(ah[:], wsm[:, 0:C_END], ACT.Copy).then_inc(s_ah, 1)
            act.wait_ge(s_w, 16 * (BLOCKS // 3 + 1))
            act.activation(wh[:, 0, 0:GU], wraw[:, 0, 0:GU], ACT.Copy).then_inc(s_guh, 1)
            act.activation(wh[:, 0, GU:WB], wraw[:, 0, GU:WB], ACT.Copy).then_inc(s_dwh, 1)

            def prep(p):
                act.wait_ge(s_ve, p + 1)
                act.activation(lnv[:], ve[:], ACT.Ln).then_inc(s_ln, 1)
                act.wait_ge(s_ln, 2 * p + 1)
                act.activation(rs[:], lnv[:], ACT.Exp, scale=-0.5).then_inc(s_ln, 1)
                for b in range(PAIRS):
                    act.wait_ge(s_xt, PAIRS * p + b + 1)
                    act.activation(xh[:, :, 2 * P * b:2 * P * (b + 1)],
                                   bank[b][:].rearrange("p (c n) -> p c n", c=HC), ACT.Copy).then_inc(s_xh, 1)

            def half_step(f, j, k, first=False):
                s = STEPS * f + 4 * j + k
                b, t = 2 * j + k // 2, k % 2
                act.wait_ge(s_g, s + 1)
                if not first:
                    act.wait_ge(s_hl, s - 3)
                act.activation(act_h[:, k, :], bank[4 + 2 * t][:], ACT.Silu).then_inc(s_silu, 1)
                act.wait_ge(s_h, s + 1)
                if not first:
                    act.wait_ge(s_down, s - 3)
                act.activation(hh[:, k, :], act_h[:, k, :], ACT.Copy).then_inc(s_hh, 1)
                r = (k // 2 + 1) % 2
                if t == 0:
                    if not (first and f == 0 and k < 2):
                        act.wait_ge(s_u, s)
                    act.activation(wh[:, r, 0:GU], block_cols(b + 1, 0, GU), ACT.Copy).then_inc(s_guh, 1)
                else:
                    if not (first and f == 0 and k < 2):
                        act.wait_ge(s_down, s - 1)
                    act.activation(wh[:, r, GU:WB], block_cols(b + 1, GU, WB), ACT.Copy).then_inc(s_dwh, 1)

            def ffn(f):
                act.wait_ge(s_logit, f + 1)
                act.activation(r8[:, 0, :], bank[1][:, 0:TT * E], ACT.Exp, scale=-1.0).then_inc(s_er, 1)
                half_step(f, 0, 0, True)
                half_step(f, 0, 1, True)
                act.wait_ge(s_cwt, f + 1)
                act.activation(cwt[:], bank[0][0:TT * E, 0:P], ACT.Copy).then_inc(s_cwc, 1)
                half_step(f, 0, 2, True)
                half_step(f, 0, 3, True)
                with act.Fori(1, BLOCKS // 2) as j:
                    for k in range(4):
                        half_step(f, j, k)

            prep(0)
            ffn(0)
            prep(1)
            for h in range(2):
                act.wait_ge(s_kp, h + 1)
                act.wait_ge(s_pads, 1)
                act.activation(kh[:, P + HALF * h:P + HALF * (h + 1)], bank[4 + h][:], ACT.Copy).then_inc(s_kh, 1)
            for n in range(2 * QG):
                act.wait_ge(s_qp, n + 1)
                if n >= 2:
                    act.wait_ge(s_qs, n - 1)
                act.activation(qh[:, n % 2, :], bank[4 + n % 2][:], ACT.Copy, scale=QK_SCALE).then_inc(s_qh, 1)
                act.activation(qb[:, n % 2, :], bank[4 + n % 2][:], ACT.Copy, scale=kinds[:, 0:1]).then_inc(s_qb, 1)

            def unit(j, k, first=False):
                u = 8 * j + k
                s = k % 2
                act.wait_ge(s_nm, u + 1)
                if not (first and k < 2):
                    act.wait_ge(s_pt, u - 1)
                for h in range(QG):
                    lo = (h % 2) * 2 * P
                    i = act.activation(prob[:, s, h * P:(h + 1) * P], bank[2 * s + h // 2][:, lo:lo + P],
                                       ACT.Exp, bias=nmax[:, s, h:h + 1])
                i.then_inc(s_exp, 1)
                if k in (2, 6) and not (first and k == 2):
                    heads_high(2 * j + (-1 if k == 2 else 0))

            def heads_high(i):
                act.wait_ge(s_ot, i + 1)
                act.activation(oh[:], bank[7][:, 0:H].rearrange("p (c n) -> p c n", c=HC), ACT.Copy).then_inc(s_oh, 1)

            for k in range(8):
                unit(0, k, True)
            with act.Fori(1, TT // 2) as j:
                for k in range(8):
                    unit(j, k)
            heads_high(TT - 1)
            prep(2)
            ffn(1)

        @block.tensor
        def _(pe):
            def prep(p):
                if p == 0:
                    pe.wait_ge(s_pool, 6)
                for b in range(PAIRS):
                    pe.wait_ge(s_xn, PAIRS * p + b + 1)
                    for c in range(HC):
                        for t in range(2):
                            at = (2 * c + t) * P
                            i = pe.transpose(bank[b][:, at:at + P], xn[:, 2 * b + t, c * P:(c + 1) * P], ident[:])
                    i.then_inc(s_xt, 1)

            def product(dst, left, right, n_left=None, first=True):
                pairs = [(0, 0), (0, 1), (1, 0)]
                chunks = len(left[0])
                for c in range(chunks):
                    for n, (a, b) in enumerate(pairs):
                        i = pe.matmul(dst, left[a][c], right[b][c], start=first and c == 0 and n == 0,
                                      stop=c == chunks - 1 and n == 2, skip_group_check=not first)
                return i

            def cols(w, at, n):
                return [w[:, at + c * n:at + (c + 1) * n] for c in range(HC)]

            def gate_up(f, j, k, first=False):
                s = STEPS * f + 4 * j + k
                t, r = k % 2, k // 2
                if t == 0:
                    pe.wait_ge(s_gul, BLOCKS * f + 2 * j + r + 1)
                if not (first and k < 2):
                    pe.wait_ge(s_h, s - 1)
                for n, sm in ((0, s_g), (1, s_u)):
                    left = [[w[:, r, (2 * n + c) * P:(2 * n + c + 1) * P] for c in range(HC)] for w in (wh, wl)]
                    right = [[v[:, c, HALF * t:HALF * (t + 1)] for c in range(HC)] for v in (xh, xl)]
                    product(bank[4 + 2 * t + n][:], left, right).then_inc(sm, 1)

            def ffn(f):
                base = STEPS * f
                for t in range(TT):
                    n = 0
                    for c in range(HC):
                        for v in (xh, xl):
                            for w in (ah, al):
                                i = pe.matmul(bank[1][:, t * E:(t + 1) * E], v[:, c, t * P:(t + 1) * P],
                                              w[:, C_RW + c * E:C_RW + (c + 1) * E], start=n == 0, stop=n == 7)
                                n += 1
                i.then_inc(s_logit, 1)
                gate_up(f, 0, 0, True)
                gate_up(f, 0, 1, True)
                pe.wait_ge(s_cw, f + 1)
                pe.transpose(bank[0][0:TT * E, 0:P], r8[:, 6, :], ident[:]).then_inc(s_cwt, 1)
                gate_up(f, 0, 2, True)
                pe.wait_ge(s_cwc, f + 1)
                for b in range(4):
                    pe.matmul(bank[b][:], zeros[:, 0:P], zeros[:], start=True, stop=False, skip_group_check=True)
                pe.wait_ge(s_dwl, BLOCKS * f + 1)
                down(f, base + 0, 1 - 1)
                gate_up(f, 0, 3, True)
                down(f, base + 1, 1)
                with pe.Fori(1, BLOCKS // 2) as j:
                    for k in range(4):
                        gate_up(f, j, k)
                        if k % 2 == 0:
                            pe.wait_ge(s_dwl, BLOCKS * f + 2 * j + k // 2)
                        down(f, base + 4 * j + k - 2, (k + 2) % 4)
                pe.wait_ge(s_dwl, BLOCKS * (f + 1))
                down(f, base + STEPS - 2, 2)
                down(f, base + STEPS - 1, 3)

            def down(f, s, k):
                t, r = k % 2, k // 2
                pe.wait_ge(s_hl, s + 1)
                for tt in range(4):
                    tile_ = 4 * t + tt
                    dst = bank[tile_ // 2][:, (tile_ % 2) * H:(tile_ % 2 + 1) * H]
                    left = [[v[:, k, tt * P:(tt + 1) * P]] for v in (hh, hl)]
                    right = [[w[:, r, GU:WB]] for w in (wh, wl)]
                    i = product(dst, left, right, first=False)
                i.then_inc(s_down, 1)

            prep(0)
            pe.wait_ge(s_xl, PAIRS)
            pe.wait_ge(s_al, 1)
            ffn(0)
            prep(1)
            pe.wait_ge(s_xl, 2 * PAIRS)
            parts = lambda at, n: [cols(w, at, n) for w in (ah, al)]
            xs = lambda a, z: [[v[:, c, a:z] for c in range(HC)] for v in (xh, xl)]
            for h in range(2):
                product(bank[4 + h][:], parts(C_WK, P), xs(HALF * h, HALF * (h + 1))).then_inc(s_kp, 1)
            for t in range(TT):
                i = product(bank[6][:, t * KV * D:(t + 1) * KV * D], xs(t * P, (t + 1) * P), parts(C_WV, KV * D))
            i.then_inc(s_vp, 1)
            for n in range(2 * QG):
                g, h = n // 2, n % 2
                if n < 2:
                    pe.wait_ge(s_kl, n + 1)
                else:
                    pe.wait_ge(s_qb, n - 1)
                left = [[w[:, C_WQ + (c * QG + g) * P:C_WQ + (c * QG + g + 1) * P] for c in range(HC)] for w in (ah, al)]
                product(bank[4 + h][:], left, xs(HALF * h, HALF * (h + 1))).then_inc(s_qp, 1)

            def scores(j, k, first):
                u, s, g, r = 8 * j + k, k % 2, k % 4, k // 4
                if g == 0:
                    pe.wait_ge(s_ring, 2 * j + r + 1)
                if not (first and k < 2):
                    pe.wait_ge(s_exp, u - 1)
                rows = slice(32 * g, 32 * (g + 1))
                for h in range(QG):
                    q = qring[rows, r, h * P:(h + 1) * P]
                    lo = (h % 2) * 2 * P
                    b = bank[2 * s + h // 2]
                    if first and r == 0:
                        pe.matmul(b[:, lo:lo + P], negs[rows, 0:P], negs[rows, P:2 * P], start=True, stop=True)
                        a, z = P, 2 * P
                    else:
                        a, z = 0, 2 * P
                    pe.matmul(b[:, lo + a:lo + z], q, khring[rows, r, a:z], start=True, stop=False)
                    i = pe.matmul(b[:, lo + a:lo + z], q, klring[rows, r, a:z], start=False, stop=True)
                i.then_inc(s_qk, 1)

            def turn(u, s, first):
                pe.wait_ge(s_exp, u + 1)
                if not first:
                    pe.wait_ge(s_pm, u - 1)
                for h in range(QG):
                    i = pe.transpose(bank[4 + s][:, h * P:(h + 1) * P], prob[:, s, h * P:(h + 1) * P], ident[:])
                i.then_inc(s_pt, 1)

            def values(i, g, s, first):
                pe.wait_ge(s_pm, 4 * i + g + 1)
                if g == 0 and not first:
                    pe.wait_ge(s_att, i)
                for h in range(QG):
                    at = (g * QG + h) * VW
                    for n, pr in ((1, pcur), (0, pprev)):
                        if isinstance(i, int):
                            v = vx[:, i + n, g, :]
                        else:
                            v = vx[:, bass.ds(i + n, 1), g, :].rearrange("p a n -> p (a n)")
                        m = pe.matmul(bank[6][:, at:at + VW], pr[:, s, h * P:(h + 1) * P], v, start=n == 1, stop=n == 0)
                m.then_inc(s_av, 1)

            def turn_out(i):
                pe.wait_ge(s_att, i + 1)
                if not (isinstance(i, int) and i == 0):
                    pe.wait_ge(s_x2, i)
                for c in range(HC):
                    m = pe.transpose(bank[7][:, c * P:(c + 1) * P], att[:, c * P:(c + 1) * P], ident[:])
                m.then_inc(s_ot, 1)

            def project(i):
                pe.wait_ge(s_ol, i + 1)
                product(bank[7][:, H:2 * H], [[v[:, c, :] for c in range(HC)] for v in (oh, ol)], parts(C_WO, H)).then_inc(s_wo, 1)

            def step(j, k, first=False):
                scores(j, k, first)
                if not (first and k == 0):
                    turn(8 * j + k - 1, (k + 1) % 2, first and k < 3)
                if not (first and k < 2):
                    i2 = 2 * j + (k - 2) // 4
                    values(i2, (k - 2) % 4, k % 2, first and k < 6)
                tail(j, k, first)

            def tail(j, k, first):
                if k in (6, 2) and not (first and k == 2):
                    turn_out(2 * j + (0 if k == 6 else -1))
                if k in (7, 3) and not (first and k == 3):
                    project(2 * j + (0 if k == 7 else -1))

            pe.wait_ge(s_pads, 2)
            pe.wait_ge(s_v, 1)
            pe.wait_ge(s_qb, 2 * QG)
            for k in range(8):
                step(0, k, True)
            with pe.Fori(1, TT // 2) as j:
                for k in range(8):
                    step(j, k)
            turn(UNITS - 1, 1, False)
            values(TT - 1, 2, 0, False)
            values(TT - 1, 3, 1, False)
            turn_out(TT - 1)
            project(TT - 1)
            pe.wait_ge(s_x2, TT)
            prep(2)
            pe.wait_ge(s_xl, 3 * PAIRS)
            ffn(1)

        @block.vector
        def _(dve):
            links = [0]

            def link(i):
                links[0] += 1
                i.then_inc(s_dve, 1)
                dve.wait_ge(s_dve, links[0])

            def prep(p):
                for t in range(TT):
                    i = dve.bn_stats(bst[:, t, :], x[:, t, :])
                link(i)
                for t in range(TT):
                    i = dve.bn_aggr(mv[:, t, :], bst[:, t, :])
                link(i)
                dve.tensor_scalar(ve[:], mv[:, :, 1], EPS, None, ALU.add).then_inc(s_ve, 1)
                dve.wait_ge(s_ln, 2 * p + 2)
                link(dve.tensor_tensor(nt[:, 0, :], ve[:], rs[:], ALU.mult))
                link(dve.tensor_tensor(nt[:, 1, :], nt[:, 0, :], rs[:], ALU.mult))
                link(dve.tensor_scalar(nt[:, 0, :], nt[:, 1, :], -0.5, 1.5, ALU.mult, ALU.add))
                link(dve.tensor_tensor(rs[:], rs[:], nt[:, 0, :], ALU.mult))
                for b in range(PAIRS):
                    for t in (2 * b, 2 * b + 1):
                        i = dve.tensor_scalar(xn[:, t, :], x[:, t, :], mv[:, t, 0:1], rs[:, t:t + 1],
                                              ALU.subtract, ALU.mult)
                    i.then_inc(s_xn, 1)
                for b in range(PAIRS):
                    dve.wait_ge(s_xh, PAIRS * p + b + 1)
                    cs = slice(2 * P * b, 2 * P * (b + 1))
                    dve.tensor_tensor(xl[:, :, cs], bank[b][:].rearrange("p (c n) -> p c n", c=HC),
                                      xh[:, :, cs].bitcast(F32), ALU.subtract).then_inc(s_xl, 1)

            def route(f):
                big = cwb[:, 2, :].rearrange("p (a n) -> p a n", a=2)
                v3 = lambda ap, n: ap.rearrange("p (t e) -> p t e", e=n)
                dve.wait_ge(s_er, f + 1)
                link(dve.tensor_scalar(r8[:, 1, :], r8[:, 0, :], 1.0, None, ALU.add))
                link(dve.reciprocal(r8[:, 2, :], r8[:, 1, :]))
                if f == 0:
                    dve.wait_ge(s_const, 48)
                    dve.wait_ge(s_pool, 6)
                sfc = v3(r8[:, 3, :], E)
                link(dve.tensor_tensor(sfc, v3(r8[:, 2, :], E), rbias[:].unsqueeze(1).to_broadcast([P, TT, E]), ALU.add))
                pairs = r8[:, 3, :].rearrange("p (g two) -> p g two", two=2)
                link(dve.tensor_tensor(r4[:, 0, :], pairs[:, :, 0], pairs[:, :, 1], ALU.add))

                def rank(vals, n, tie, above, equal, dst):
                    for t in range(TT):
                        a = vals[:, t, :].unsqueeze(2).to_broadcast([P, n, n])
                        b = vals[:, t, :].unsqueeze(1).to_broadcast([P, n, n])
                        sl = slice(t * n * n, (t + 1) * n * n)
                        g = above[:, sl].rearrange("p (i j) -> p i j", j=n)
                        q = equal[:, sl].rearrange("p (i j) -> p i j", j=n)
                        dve.tensor_tensor(g, b, a, ALU.is_gt)
                        i = dve.tensor_tensor(q, b, a, ALU.is_equal)
                    link(i)
                    q = equal.rearrange("p (t m) -> p t m", t=TT)
                    link(dve.tensor_tensor(q, q, tie[:].rearrange("p i j -> p (i j)").unsqueeze(1).to_broadcast([P, TT, n * n]), ALU.mult))
                    link(dve.tensor_tensor(above, above, equal, ALU.add))
                    link(dve.tensor_reduce(dst, above.rearrange("p (m j) -> p m j", j=n), AX_X, ALU.add))

                rank(v3(r4[:, 0, :], NG), NG, tie4, r16[:, 0, :], r16[:, 1, :], r4[:, 1, :])
                link(dve.tensor_scalar(r4[:, 2, :], r4[:, 1, :], 2.0, None, ALU.is_lt))
                gm = r4[:, 2, :].unsqueeze(2).to_broadcast([P, TT * NG, 2])
                link(dve.tensor_tensor(r8[:, 4, :].rearrange("p (g two) -> p g two", two=2), pairs, gm, ALU.mult))
                rank(v3(r8[:, 4, :], E), E, tie8, big[:, 0, :], big[:, 1, :], r8[:, 5, :])
                link(dve.tensor_scalar(r8[:, 5, :], r8[:, 5, :], 2.0, None, ALU.is_lt))
                link(dve.tensor_tensor(r8[:, 5, :], r8[:, 5, :], r8[:, 2, :], ALU.mult))
                link(dve.tensor_reduce(r4[:, 3, 0:TT], v3(r8[:, 5, :], E), AX_X, ALU.add))
                link(dve.tensor_scalar(r4[:, 3, 0:TT], r4[:, 3, 0:TT], 1e-20, None, ALU.add))
                link(dve.reciprocal(r4[:, 3, TT:2 * TT], r4[:, 3, 0:TT]))
                link(dve.tensor_scalar(r4[:, 3, TT:2 * TT], r4[:, 3, TT:2 * TT], SCALE, None, ALU.mult))
                cw = r8[:, 6, :].rearrange("p (e t) -> p t e", e=E)
                dve.tensor_tensor(cw, v3(r8[:, 5, :], E), r4[:, 3, TT:2 * TT].unsqueeze(2).to_broadcast([P, TT, E]),
                                  ALU.mult).then_inc(s_cw, 1)


            def half_step(f, j, k, row):
                s = STEPS * f + 4 * j + k
                t = k % 2
                h = act_h[:, k, :]
                u = bank[5 + 2 * t]
                dve.wait_ge(s_silu, s + 1)
                dve.tensor_tensor(h, h, row(t), ALU.mult).then_inc(s_cwm, 1)
                dve.wait_ge(s_cwm, s + 1)
                dve.wait_ge(s_u, s + 1)
                dve.tensor_tensor(h, u[:], h, ALU.mult).then_inc(s_h, 1)
                dve.wait_ge(s_hh, s + 1)
                dve.tensor_tensor(hl[:, k, :], h, hh[:, k, :].bitcast(F32), ALU.subtract).then_inc(s_hl, 1)

            def ffn(f):
                route(f)
                dve.wait_ge(s_ones, f + 1)

                def row_of(b):
                    def row(t):
                        if isinstance(b, int):
                            return cwb[:, b, HALF * t:HALF * (t + 1)]
                        return cwb[:, bass.ds(b, 1), HALF * t:HALF * (t + 1)].rearrange("p a n -> p (a n)")
                    return row

                for k in range(4):
                    half_step(f, 0, k, row_of(0))
                half_step(f, 1, 0, row_of(0))
                half_step(f, 1, 1, row_of(0))
                dve.wait_ge(s_cwb, 16 * N_CWB * (f + 1))
                half_step(f, 1, 2, row_of(1))
                half_step(f, 1, 3, row_of(1))
                with dve.Fori(2, BLOCKS // 2) as j:
                    for k in range(4):
                        half_step(f, j, k, row_of(2 * j + k // 2 - 2))
                dve.wait_ge(s_down, STEPS * (f + 1))
                for b in range(PAIRS):
                    xs = x[:, 2 * b:2 * b + 2, :].rearrange("p t h -> p (t h)")
                    i = dve.scalar_tensor_tensor(out=xs, in0=bank[b][:], scalar=0.5, in1=xs, op0=ALU.mult, op1=ALU.add)
                    i.then_inc(s_fin, 1)
                dve.wait_ge(s_fin, PAIRS * (f + 1))

            dve.wait_ge(s_x, 32)
            prep(0)
            ffn(0)
            prep(1)
            for h in range(2):
                dve.wait_ge(s_kh, h + 1)
                cs = slice(P + HALF * h, P + HALF * (h + 1))
                dve.tensor_tensor(kl[:, cs], bank[4 + h][:], kh[:, cs].bitcast(F32), ALU.subtract).then_inc(s_kl, 1)
            dve.wait_ge(s_vp, 1)
            dve.tensor_copy(vx[:, 1:TT + 1, :, 0:D], bank[6][:].rearrange("p (t g d) -> p t g d", t=TT, g=KV)).then_inc(s_v, 1)
            for n in range(2 * QG):
                dve.wait_ge(s_qb, n + 1)
                dve.scalar_tensor_tensor(out=qs[:, n // 2, HALF * (n % 2):HALF * (n % 2 + 1)],
                                         in0=qh[:, n % 2, :].bitcast(F32), scalar=kinds[:, 1:2], in1=qb[:, n % 2, :],
                                         op0=ALU.mult, op1=ALU.add).then_inc(s_qs, 1)

            def pick_max(j, k):
                u, s = 8 * j + k, k % 2
                dve.wait_ge(s_qk, u + 1)
                dve.memset(idle[:], 0.0)
                for b in range(2):
                    v = bank[2 * s + b][:].rearrange("p (h w k) -> p h w k", h=2, w=2)
                    i = dve.copy_predicated(v[:, :, 0, :], sel_q[:, 2 * b:2 * b + 2, :].bitcast(I32), v[:, :, 1, :])
                i.then_inc(s_sel, 1)
                dve.wait_ge(s_sel, u + 1)
                for b in range(2):
                    v = bank[2 * s + b][:].rearrange("p (h w k) -> p h w k", h=2, w=2)
                    i = dve.tensor_reduce(nmax[:, s, 2 * b:2 * b + 2], v[:, :, 0, :], AX_X, ALU.max, negate=True)
                i.then_inc(s_nm, 1)

            def split_probs(u, s, first):
                dve.wait_ge(s_pt, u + 1)
                if not first:
                    dve.wait_ge(s_av, u - 1)
                p = bank[4 + s]
                dve.tensor_tensor(pcur[:, s, :], p[:], cur_k[:].rearrange("p h q -> p (h q)"), ALU.mult)
                dve.tensor_tensor(pprev[:, s, :], p[:], prev_k[:].rearrange("p h q -> p (h q)"), ALU.mult).then_inc(s_pm, 1)

            def normalise(i):
                dve.wait_ge(s_av, 4 * i + 4)
                if not (isinstance(i, int) and i == 0):
                    dve.wait_ge(s_ot, i)
                o = bank[6][:, 0:HEADS * VW].rearrange("p (h d) -> p h d", d=VW)
                dve.reciprocal(rden[:], o[:, :, D]).then_inc(s_rd, 1)
                dve.wait_ge(s_rd, i + 1)
                dve.tensor_tensor(att[:].rearrange("p (h d) -> p h d", d=D), o[:, :, 0:D],
                                  rden[:].unsqueeze(2).to_broadcast([P, HEADS, D]), ALU.mult).then_inc(s_att, 1)

            def heads_low(i):
                dve.wait_ge(s_oh, i + 1)
                dve.tensor_tensor(ol[:], bank[7][:, 0:H].rearrange("p (c n) -> p c n", c=HC), oh[:].bitcast(F32),
                                  ALU.subtract).then_inc(s_ol, 1)

            def add_heads(i):
                dve.wait_ge(s_wo, i + 1)
                xs = x[:, i, :] if isinstance(i, int) else x[:, bass.ds(i, 1), :].rearrange("p a n -> p (a n)")
                dve.tensor_tensor(xs, bank[7][:, H:2 * H], xs, ALU.add).then_inc(s_x2, 1)

            def step(j, k, first=False):
                pick_max(j, k)
                if not (first and k == 0):
                    split_probs(8 * j + k - 1, (k + 1) % 2, first and k < 3)
                for c, act_on in ((5, normalise), (6, heads_low), (7, add_heads)):
                    if k == c:
                        act_on(2 * j)
                    if k == c - 4 and not first:
                        act_on(2 * j - 1)

            dve.wait_ge(s_pads, 2)
            dve.wait_ge(s_xb, TT)
            for k in range(8):
                step(0, k, True)
            with dve.Fori(1, TT // 2) as j:
                for k in range(8):
                    step(j, k)
            split_probs(UNITS - 1, 1, False)
            normalise(TT - 1)
            heads_low(TT - 1)
            add_heads(TT - 1)
            dve.wait_ge(s_x2, TT)
            dve.memset(cwb[:, 0, :], 1.0).then_inc(s_ones, 1)
            prep(2)
            ffn(1)


def _lay_out(np, a):
    def hidden_rows(shared, routed):
        pad = np.zeros((SH_BLOCKS * P - I_SHARED, H), np.float32)
        rows = np.concatenate([shared, pad, routed.reshape(E * I_MOE, H)])
        return rows.reshape(BLOCKS, P, H)

    gate = hidden_rows(a["L0_ffn_shared_gate_w"], a["L0_ffn_gate_w"]).reshape(BLOCKS, P, HC, P)
    up = hidden_rows(a["L0_ffn_shared_up_w"], a["L0_ffn_up_w"]).reshape(BLOCKS, P, HC, P)
    down = hidden_rows(a["L0_ffn_shared_down_w"].T, a["L0_ffn_down_w"].transpose(0, 2, 1))
    to_cols = lambda w: w.transpose(3, 0, 2, 1).reshape(P, BLOCKS, HC * P)
    blocks = np.concatenate([to_cols(gate), to_cols(up), down.transpose(1, 0, 2)], axis=2)
    blocks = np.concatenate([blocks, blocks[:, 0:1]], axis=1)

    wq = a["L0_attn_Wq"].reshape(HC, P, KV, QG, 1, D)
    wq = np.concatenate([wq, wq], axis=4).transpose(1, 0, 3, 2, 4, 5).reshape(P, HC * QG * P)
    wk = a["L0_attn_Wk"].reshape(HC, P, KV, 1, D)
    wk = np.concatenate([wk, wk], axis=3).transpose(1, 0, 2, 3, 4).reshape(P, HC * P)
    wv = a["L0_attn_Wv"].reshape(HC, P, KV * D).transpose(1, 0, 2).reshape(P, HC * KV * D)
    wo = a["L0_attn_Wo"].reshape(HC, P, H).transpose(1, 0, 2).reshape(P, HC * H)
    rw = a["L0_ffn_router_weight"].T.reshape(HC, P, E).transpose(1, 0, 2).reshape(P, HC * E)
    small = np.concatenate([wq, wk, wv, wo, rw], axis=1)

    kinds = np.zeros((P // (2 * D), 2, D, 2), np.float32)
    kinds[:, 0, :, 1] = 1.0
    kinds[:, 1, :, 0] = QK_SCALE
    kinds[:, 1, :, 1] = -1.0
    return {
        "x_in": a["L0_attn_x"], "w_blocks": blocks, "w_small": small, "row_kind": kinds.reshape(P, 2),
        "router_bias": a["L0_ffn_e_score_correction_bias"], "out_bias": a["L0_attn_bo"],
    }


def kernel(**inputs):
    import numpy as np
    import concourse.bacc as bacc
    from concourse import mybir as _mybir
    from concourse.bass_utils import run_bass_kernel_spmd as run

    nc = bacc.Bacc("TRN2", target_bir_lowering=False, num_devices=1)
    arrays = {k: np.ascontiguousarray(v) for k, v in _lay_out(np, {k: np.asarray(v) for k, v in inputs.items()}).items()}
    args = [nc.dram_tensor(k, v.shape, _mybir.dt.from_np(v.dtype), kind="ExternalInput").ap() for k, v in arrays.items()]
    out = nc.dram_tensor("out_dram", (1, T, H), F32, kind="ExternalOutput").ap()
    macaron_kernel(nc, *args, out)
    return run(nc, [arrays], core_ids=[0]).results[0]["out_dram"]
```

```python
from contextlib import ExitStack

import concourse.bass as bass
from concourse import mybir

F32 = mybir.dt.float32
F32R = mybir.dt.float32r
BF16 = mybir.dt.bfloat16
I32 = mybir.dt.int32
ALU = mybir.AluOpType
ACT = mybir.ActivationFunctionType
AX_X = mybir.AxisListType.X

P = 128
T = 1024
TT = T // P
H = 256
HC = H // P
E = 8
NG = 4
I_MOE = 176
I_SHARED = 352
SH_BLOCKS = -(-I_SHARED // P)
RT_BLOCKS = E * I_MOE // P
BLOCKS = SH_BLOCKS + RT_BLOCKS
HALF = 512
STEPS = 2 * BLOCKS
WARM = 18
LAST = BLOCKS - 2
GU = 4 * P
WB = GU + H
SCALE = 2.5
EPS = 1e-5

HEADS = 16
KV = 4
QG = HEADS // KV
D = 16
UNITS = TT * KV
QK_SCALE = 0.25
NEG = -1e30
GR = 2 * D

C_WQ = 0
C_WK = C_WQ + HC * QG * P
C_WV = C_WK + HC * P
C_WO = C_WV + HC * KV * D
C_RW = C_WO + QG * H
C_END = C_RW + HC * E


def macaron_kernel(nc, x_in, w_blocks, w_small, row_kind, router_bias, out_bias, out):
    with ExitStack() as ctx:
        def sb(name, shape, dt=F32, stack=ctx):
            return stack.enter_context(nc.sbuf_tensor(name, shape, dt))

        def sem(name):
            return ctx.enter_context(nc.semaphore(name))

        psum = ctx.enter_context(nc.psum_tensor("psum", [P, 8, 512], F32))
        bank = [psum[:, i, :] for i in range(8)]

        x = sb("x", [P, TT, H])
        xh = sb("xh", [P, HC, T], F32R)
        xl = sb("xl", [P, HC, T], F32R)
        wraw = sb("wraw", [P, BLOCKS, WB])
        wh = sb("wh", [P, 2, WB], F32R)
        wl = sb("wl", [P, 2, WB], F32R)
        ah = sb("ah", [P, C_RW], F32R)
        al = sb("al", [P, C_RW], F32R)
        rw = sb("rw", [P, HC, 2, E], F32R)
        ident = sb("ident", [P, P])
        zeros = sb("zeros", [P, 512], BF16)
        negs = sb("negs", [P, 2 * P], BF16)
        sel_q = sb("sel_q", [P, 2, P])
        vprev = sb("vprev", [P, 2, KV * (P + GR)], F32R)
        vdiff = sb("vdiff", [P, 2, KV * (P + GR)], F32R)
        kinds = sb("kinds", [P, 2])
        rbias = sb("rbias", [P, E])
        obias = sb("obias", [P, H])
        bst = sb("bst", [P, TT, 6])
        mv = sb("mv", [P, TT, 2])
        ve = sb("ve", [P, TT])
        lnv = sb("lnv", [P, TT])
        rs = sb("rs", [P, TT])
        nt = sb("nt", [P, 2, TT])
        r8 = sb("r8", [P, 8, TT * E])
        r4 = sb("r4", [P, 4, TT * NG])
        r16 = sb("r16", [P, 2, TT * NG * NG])
        tie4 = sb("tie4", [P, NG, NG])
        tie8 = sb("tie8", [P, E, E])
        cwt = sb("cwt", [TT * E, P])
        with ExitStack() as ffn_stack:
            cwb = sb("cwb", [P, RT_BLOCKS + 1, T], F32, ffn_stack)
            act_h = sb("act_h", [P, 4, HALF], F32, ffn_stack)
            hh = sb("hh", [P, 4, HALF], F32R, ffn_stack)
            hl = sb("hl", [P, 4, HALF], F32R, ffn_stack)
        with ExitStack() as attn_stack:
            qs = sb("qs", [P, QG, T], F32R, attn_stack)
            qh = sb("qh", [P, 2, HALF], F32R, attn_stack)
            qb = sb("qb", [P, 2, HALF], F32, attn_stack)
            kh = sb("kh", [P, T], F32R, attn_stack)
            kl = sb("kl", [P, T], F32R, attn_stack)
            qring = sb("qring", [P, 2, QG * P], F32R, attn_stack)
            khring = sb("khring", [P, 2, 2 * P], F32R, attn_stack)
            klring = sb("klring", [P, 2, 2 * P], F32R, attn_stack)
            vf = sb("vf", [P, TT + 1, KV, D], F32, attn_stack)
            vd = sb("vd", [P, TT, KV, D], F32, attn_stack)
            vc = sb("vc", [P, TT + 1, KV, GR], F32R, attn_stack)
            vdc = sb("vdc", [P, TT, KV, GR], F32R, attn_stack)
            nmax = sb("nmax", [P, 2, QG], F32, attn_stack)
            prob = sb("prob", [P, 2, QG * P], F32, attn_stack)
            pall = sb("pall", [P, 2, 2, QG * P], F32R, attn_stack)
            pcur = sb("pcur", [P, 2, 2, QG * P], F32R, attn_stack)
            idle_p = sb("idle_p", [P, 4], F32, attn_stack)
            idle = sb("idle", [P, 4], F32, attn_stack)
            psums = sb("psums", [P, 2, KV, QG], F32, attn_stack)
            rsums = sb("rsums", [P, KV, QG], F32, attn_stack)
            rexp = sb("rexp", [P, QG, KV, GR], F32, attn_stack)
            rden = sb("rden", [P, QG * P], F32, attn_stack)
            att = sb("att", [P, QG * P], F32, attn_stack)
            oh = sb("oh", [P, QG * P], F32R, attn_stack)
            ol = sb("ol", [P, QG * P], F32R, attn_stack)
        wsm = cwb[:, RT_BLOCKS - 2:RT_BLOCKS + 1, :].rearrange("p a b -> p (a b)")
        xn = act_h[:, :, :].rearrange("p a (b n) -> p (a b) n", n=H)
        cw_dram = nc.dram_tensor("cw_dram", (TT * E, P), F32, kind="Internal").ap()

        s_x = [sem(f"s_x{k}") for k in range(2)]
        s_w = [sem(f"s_w{k}") for k in range(3)]
        s_small = sem("s_small")
        s_router = sem("s_router")
        s_rh = sem("s_rh")
        s_rl = sem("s_rl")
        s_const = sem("s_const")
        s_pool = sem("s_pool")
        s_zeros = sem("s_zeros")
        s_ah = sem("s_ah")
        s_al = sem("s_al")
        s_dve = sem("s_dve")
        s_ve = sem("s_ve")
        s_ln = sem("s_ln")
        s_rs = sem("s_rs")
        s_xn = sem("s_xn")
        s_xt = sem("s_xt")
        s_xh = sem("s_xh")
        s_xl = sem("s_xl")
        s_lp = sem("s_lp")
        s_logit = sem("s_logit")
        s_er = sem("s_er")
        s_cw = sem("s_cw")
        s_cwt = sem("s_cwt")
        s_cwc = sem("s_cwc")
        s_cwd = sem("s_cwd")
        s_cwb = [sem(f"s_cwb{k}") for k in range(3)]
        s_ones = sem("s_ones")
        s_guh = sem("s_guh")
        s_gul = sem("s_gul")
        s_dwh = sem("s_dwh")
        s_dwl = sem("s_dwl")
        s_g = sem("s_g")
        s_u = sem("s_u")
        s_silu = sem("s_silu")
        s_cwm = sem("s_cwm")
        s_h = sem("s_h")
        s_hh = sem("s_hh")
        s_hl = sem("s_hl")
        s_down = sem("s_down")
        s_fin = sem("s_fin")
        s_xb = sem("s_xb")
        s_kp = sem("s_kp")
        s_kh = sem("s_kh")
        s_kl = sem("s_kl")
        s_vp = sem("s_vp")
        s_v = sem("s_v")
        s_qp = sem("s_qp")
        s_qh = sem("s_qh")
        s_qb = sem("s_qb")
        s_qd = sem("s_qd")
        s_qs = sem("s_qs")
        s_pads = sem("s_pads")
        s_ring = [sem(f"s_ring{k}") for k in range(2)]
        s_qk = [sem(f"s_qk{k}") for k in range(2)]
        s_sel = sem("s_sel")
        s_nm = sem("s_nm")
        s_exp = sem("s_exp")
        s_pt = sem("s_pt")
        s_pah = sem("s_pah")
        s_pal = sem("s_pal")
        s_pm = sem("s_pm")
        s_vz = sem("s_vz")
        s_vd = sem("s_vd")
        s_vch = sem("s_vch")
        s_vcl = sem("s_vcl")
        s_vr = [sem(f"s_vr{k}") for k in range(2)]
        s_av = sem("s_av")
        s_rd = sem("s_rd")
        s_rexp = sem("s_rexp")
        s_rt = sem("s_rt")
        s_rden = sem("s_rden")
        s_att = sem("s_att")
        s_oh = sem("s_oh")
        s_ol = sem("s_ol")
        s_wo = sem("s_wo")
        s_x2 = sem("s_x2")
        s_out = sem("s_out")
        PAIRS = TT // 2

        block = ctx.enter_context(nc.Block())

        def small_part(k):
            return slice(k * C_RW // 3, (k + 1) * C_RW // 3)

        def block_cols(b, a, z):
            if isinstance(b, int):
                return wraw[:, b, a:z]
            return wraw[:, bass.ds(b, 1), a:z].rearrange("p a n -> p (a n)")

        def diagonal(v, k):
            return v[:, k, :].rearrange("p (g n) -> p g n", g=KV)[:, :, 0:GR]

        def expert_runs(b):
            at, runs = 0, []
            while at < P:
                e = (b * P + at) // I_MOE
                n = min(P - at, (e + 1) * I_MOE - b * P - at)
                runs.append((at, n, e))
                at += n
            return runs

        def stage_of(b):
            return (b > 0) + (b > 4)

        N_CWB = [sum(len(expert_runs(b)) for b in range(RT_BLOCKS) if stage_of(b) == k) for k in range(3)]

        @block.sync
        def _(sp):
            x_tiles = x_in.rearrange("a (t p) h -> p (a t) h", p=P)
            sp.dma_start(x[:, 0:4, :], x_tiles[:, 0:4, :]).then_inc(s_x[0], 16)
            sp.dma_start(wraw[:, 0, :], w_blocks[:, 0, :]).then_inc(s_w[0], 16)
            sp.dma_start(x[:, 4:8, :], x_tiles[:, 4:8, :]).then_inc(s_x[1], 16)
            sp.dma_start(wraw[:, 1, :], w_blocks[:, 1, :]).then_inc(s_w[1], 16)
            sp.dma_start(wsm[:, C_RW:C_END], w_small[:, C_RW:C_END]).then_inc(s_router, 16)
            sp.dma_start(kinds[:], row_kind).then_inc(s_const, 16)
            sp.dma_start(rbias[:], router_bias.partition_broadcast(P)).then_inc(s_const, 16)
            sp.dma_start(obias[:], out_bias.partition_broadcast(P)).then_inc(s_const, 16)
            sp.dma_start(wsm[:, 0:C_RW], w_small[:, 0:C_RW]).then_inc(s_small, 16)
            for b in range(2, BLOCKS, 3):
                sp.dma_start(wraw[:, b:b + 3, :], w_blocks[:, b:b + 3, :]).then_inc(s_w[2], 16)

            def combine_weights(f):
                sp.wait_ge(s_cwc, f + 1)
                sp.dma_start(cw_dram, cwt[:]).then_inc(s_cwd, 16)
                sp.wait_ge(s_cwd, 16 * (f + 1))
                rows = cw_dram.rearrange("(e t) p -> e (t p)", e=E)
                for b in range(RT_BLOCKS):
                    if f == 0 and b == RT_BLOCKS - 3:
                        sp.wait_ge(s_al, 3)
                    for at, n, e in expert_runs(b):
                        sp.dma_start(cwb[at:at + n, b + 1, :], rows[e, :].partition_broadcast(n)).then_inc(s_cwb[stage_of(b)], 16)
            def to_places(i, k, first=False):
                if not first:
                    sp.wait_ge(s_qs, 2 * QG)
                    sp.wait_ge(s_kl, 2)
                    sp.wait_ge(s_qk[1], 4 * i - 4)
                alone = isinstance(i, int) and i == 0
                a = P if alone else 0
                w = slice(0, P) if alone else bass.ds(i * P - P, 2 * P)
                sp.dma_start(qring[:, k, :].rearrange("p (h q) -> p h q", h=QG).bitcast(F32), qs[:, :, bass.ds(i * P, P)].bitcast(F32)).then_inc(s_ring[k], 16)
                sp.dma_start(khring[:, k, a:2 * P].bitcast(F32), kh[:, w].bitcast(F32)).then_inc(s_ring[k], 16)
                sp.dma_start(klring[:, k, a:2 * P].bitcast(F32), kl[:, w].bitcast(F32)).then_inc(s_ring[k], 16)
                if not first:
                    sp.wait_ge(s_vcl, 4)
                    sp.wait_ge(s_av, 4 * i - 4)
                for dst, src in ((vprev, vc), (vdiff, vdc)):
                    v = src[:, bass.ds(i, 1), :, :].rearrange("p a g w -> p (a g) w")
                    sp.dma_start(diagonal(dst, k).bitcast(F32), v.bitcast(F32)).then_inc(s_vr[k], 16)

            combine_weights(0)
            sp.wait_ge(s_qs, QG)
            sp.wait_ge(s_kl, 1)
            sp.wait_ge(s_vcl, 2)
            to_places(0, 0, True)
            to_places(1, 1, True)
            with sp.Fori(1, TT // 2) as j:
                for k in range(2):
                    to_places(2 * j + k, k)
            combine_weights(1)
            out_tiles = out.rearrange("a (t p) h -> p (a t) h", p=P)
            for b in range(PAIRS):
                sp.wait_ge(s_fin, PAIRS + b + 1)
                sp.dma_start(out_tiles[:, 2 * b:2 * b + 2, :], x[:, 2 * b:2 * b + 2, :]).then_inc(s_out, 16)
            sp.wait_ge(s_out, 16 * PAIRS)

        @block.gpsimd
        def _(pool):
            pool.memset(ident[:], 0.0).then_inc(s_pool, 1)
            pool.memset(zeros[:], 0.0).then_inc(s_zeros, 1)
            pool.memset(negs[:, 0:P], 1.0 / 32)
            pool.memset(negs[:, P:2 * P], NEG)
            pool.memset(tie4[:], 1.0).then_inc(s_pool, 1)
            pool.memset(tie8[:], 1.0).then_inc(s_pool, 1)
            pool.wait_ge(s_pool, 3)
            pool.affine_select(out=ident[:], in_=ident[:], compare_op=ALU.not_equal, fill=1.0, base=0,
                               pattern=[[-1, P]], channel_multiplier=1).then_inc(s_pool, 1)
            pool.affine_select(out=tie4[:], in_=tie4[:], compare_op=ALU.is_gt, fill=0.0, base=0,
                               pattern=[[1, NG], [-1, NG]], channel_multiplier=0).then_inc(s_pool, 1)
            pool.affine_select(out=tie8[:], in_=tie8[:], compare_op=ALU.is_gt, fill=0.0, base=0,
                               pattern=[[1, E], [-1, E]], channel_multiplier=0).then_inc(s_pool, 1)
            pool.memset(sel_q[:], 1.0)
            pool.memset(vprev[:].bitcast(F32), 0.0)
            pool.memset(vdiff[:].bitcast(F32), 0.0).then_inc(s_pads, 1)
            pool.wait_ge(s_pads, 1)
            pool.affine_select(out=sel_q[:], in_=sel_q[:], compare_op=ALU.is_ge, fill=0.0, base=0,
                               pattern=[[0, 2], [-1, P]], channel_multiplier=1).then_inc(s_pads, 1)
            def low_gate_up(b, r, n):
                pool.wait_ge(s_guh, n)
                pool.tensor_tensor(wl[:, r, 0:GU], block_cols(b, 0, GU), wh[:, r, 0:GU].bitcast(F32),
                                   ALU.subtract).then_inc(s_gul, 1)

            def low_down(b, r, n):
                pool.wait_ge(s_dwh, n)
                pool.tensor_tensor(wl[:, r, GU:WB], block_cols(b, GU, WB), wh[:, r, GU:WB].bitcast(F32),
                                   ALU.subtract).then_inc(s_dwl, 1)

            def first_low_parts(f):
                for b in range(2):
                    low_gate_up(b, b, BLOCKS * f + b + 1)
                    low_down(b, b, BLOCKS * f + b + 1)

            def low_parts(f):
                n = BLOCKS * f + 1
                low_gate_up(2, 0, n + 2)
                with pool.Fori(1, LAST // 2) as j:
                    for k in range(2):
                        low_gate_up(2 * j + k + 1, 1 - k, n + 2 * j + k + 1)
                        low_down(2 * j + k, k, n + 2 * j + k)
                low_gate_up(LAST + 1, 1, n + LAST + 1)
                low_down(LAST, 0, n + LAST)
                low_down(LAST + 1, 1, n + LAST + 1)

            pool.memset(cwb[:, 0, :], 1.0).then_inc(s_ones, 1)
            first_low_parts(0)
            pool.wait_ge(s_rh, 1)
            pool.tensor_tensor(rw[:, :, 1, :], wsm[:, C_RW:C_END].rearrange("p (c e) -> p c e", c=HC),
                               rw[:, :, 0, :].bitcast(F32), ALU.subtract).then_inc(s_rl, 1)
            for k in range(3):
                pool.wait_ge(s_ah, k + 1)
                w = small_part(k)
                pool.tensor_tensor(al[:, w], wsm[:, w], ah[:, w].bitcast(F32), ALU.subtract).then_inc(s_al, 1)
            low_parts(0)

            pool.memset(vf[:, 0, :, :], 0.0)
            pool.memset(vc[:, 0, :, :].bitcast(F32), 0.0).then_inc(s_vz, 1)
            pool.wait_ge(s_vz, 1)
            for h in range(2):
                a, z = h * TT // 2, (h + 1) * TT // 2
                pool.wait_ge(s_v, h + 1)
                pool.tensor_tensor(vd[:, a:z], vf[:, a + 1:z + 1, :, :], vf[:, a:z, :, :], ALU.subtract).then_inc(s_vd, 1)
                pool.wait_ge(s_vch, 2 * h + 1)
                pool.tensor_tensor(vc[:, a + 1:z + 1, :, D:GR], vf[:, a + 1:z + 1, :, :],
                                   vc[:, a + 1:z + 1, :, 0:D].bitcast(F32), ALU.subtract).then_inc(s_vcl, 1)
                pool.wait_ge(s_vch, 2 * h + 2)
                pool.tensor_tensor(vdc[:, a:z, :, D:GR], vd[:, a:z], vdc[:, a:z, :, 0:D].bitcast(F32),
                                   ALU.subtract).then_inc(s_vcl, 1)
            first_low_parts(1)
            pool.wait_ge(s_const, 48)

            def own_tile(j, k, first=False):
                u, s = 8 * j + k, k % 2
                if not (first and k < 2):
                    pool.wait_ge(s_av, u - 1)
                for w, there in ((0, s_pah), (1, s_pal)):
                    pool.wait_ge(there, u + 1)
                    pool.tensor_tensor(idle_p[:, 2 * s + w:2 * s + w + 1], kinds[:, 0:1], kinds[:, 1:2], ALU.add)
                    pool.affine_select(out=pcur[:, s, w, :].rearrange("p (h q) -> p h q", h=QG),
                                       in_=pall[:, s, w, :].rearrange("p (h q) -> p h q", h=QG),
                                       compare_op=ALU.is_ge, fill=0.0, base=0,
                                       pattern=[[0, QG], [1, P]], channel_multiplier=-1).then_inc(s_pm, 1)

            def heads_low(i):
                pool.wait_ge(s_oh, i + 1)
                if not (isinstance(i, int) and i == 0):
                    pool.wait_ge(s_wo, i)
                pool.tensor_tensor(ol[:], att[:], oh[:].bitcast(F32), ALU.subtract).then_inc(s_ol, 1)
                xs = x[:, i, :] if isinstance(i, int) else x[:, bass.ds(i, 1), :].rearrange("p a n -> p (a n)")
                pool.tensor_tensor(xs, xs, obias[:], ALU.add).then_inc(s_xb, 1)

            def unit_pair(j, first=False):
                for k in range(8):
                    if k == 6:
                        heads_low(2 * j)
                    if k == 2 and not first:
                        heads_low(2 * j - 1)
                    own_tile(j, k, first)

            unit_pair(0, True)
            with pool.Fori(1, TT // 2) as j:
                unit_pair(j)
            heads_low(TT - 1)
            low_parts(1)

        @block.scalar
        def _(act):
            def inv_std(p, h):
                ts = slice(h * TT // 2, (h + 1) * TT // 2)
                act.wait_ge(s_ve, 2 * p + h + 1)
                act.activation(lnv[:, ts], ve[:, ts], ACT.Ln).then_inc(s_ln, 1)
                act.wait_ge(s_ln, 4 * p + 2 * h + 1)
                act.activation(rs[:, ts], lnv[:, ts], ACT.Exp, scale=-0.5).then_inc(s_ln, 1)

            def highs(p, h):
                for b in (2 * h, 2 * h + 1):
                    act.wait_ge(s_xt, PAIRS * p + b + 1)
                    act.activation(xh[:, :, 2 * P * b:2 * P * (b + 1)],
                                   bank[b].rearrange("p (c n) -> p c n", c=HC), ACT.Copy).then_inc(s_xh, 1)

            def high_gate_up(b, r, last):
                if last is not None:
                    act.wait_ge(s_u, last + 1)
                act.activation(wh[:, r, 0:GU], block_cols(b, 0, GU), ACT.Copy).then_inc(s_guh, 1)

            def high_down(b, r, last):
                if last is not None:
                    act.wait_ge(s_down, last + 1)
                act.activation(wh[:, r, GU:WB], block_cols(b, GU, WB), ACT.Copy).then_inc(s_dwh, 1)

            def half_step(f, j, k, first=False, last=False):
                s = STEPS * f + 4 * j + k
                act.wait_ge(s_g, s + 1)
                if not first:
                    act.wait_ge(s_hl, s - 3)
                act.activation(act_h[:, k, :], bank[4 + 2 * (k % 2)], ACT.Silu).then_inc(s_silu, 1)
                if first:
                    if k == 3:
                        high_gate_up(2, 0, s - 1)
                elif last:
                    if k == 0:
                        high_gate_up(LAST + 1, 1, s - 1)
                elif k % 2 == 0:
                    high_gate_up(2 * j + k // 2 + 1, (k // 2 + 1) % 2, s - 1)
                if last and k == 3 and f == 0:
                    act.preload_act_table_set("natural_log_exp_and_others")
                act.wait_ge(s_h, s + 1)
                if not first:
                    act.wait_ge(s_down, s - 3)
                act.activation(hh[:, k, :], act_h[:, k, :], ACT.Copy).then_inc(s_hh, 1)
                if last:
                    if k < 2:
                        high_down(LAST + k, k, s - 2)
                elif k % 2 == 0 and not first:
                    high_down(2 * j + k // 2, k // 2, s - 2)

            def first_blocks(f, b):
                if f == 0:
                    act.wait_ge(s_w[b], 16)
                high_gate_up(b, b, STEPS * f - 2 + b if f else None)
                high_down(b, b, STEPS * f - 2 + b if f else None)

            def ffn(f):
                def split_small(k):
                    if f == 0:
                        act.activation(ah[:, small_part(k)], wsm[:, small_part(k)], ACT.Copy).then_inc(s_ah, 1)

                half_step(f, 0, 0, first=True)
                if f == 0:
                    act.wait_ge(s_small, 16)
                split_small(0)
                half_step(f, 0, 1, first=True)
                split_small(1)
                act.wait_ge(s_logit, f + 1)
                act.activation(r8[:, 0, :], r8[:, 1, :], ACT.Exp, scale=-1.0).then_inc(s_er, 1)
                half_step(f, 0, 2, first=True)
                split_small(2)
                if f == 0:
                    act.wait_ge(s_w[2], 16 * 4)
                half_step(f, 0, 3, first=True)
                half_step(f, 1, 0)
                act.wait_ge(s_cwt, f + 1)
                act.activation(cwt[:], bank[7][0:TT * E, 0:P], ACT.Copy).then_inc(s_cwc, 1)
                for k in range(1, 4):
                    half_step(f, 1, k)
                with act.Fori(2, LAST // 2) as j:
                    for k in range(4):
                        half_step(f, j, k)
                for k in range(4):
                    half_step(f, LAST // 2, k, last=True)

            act.preload_act_table_set("natural_log_exp_and_others")
            for h in range(2):
                inv_std(0, h)
                first_blocks(0, h)
                highs(0, h)
            act.wait_ge(s_router, 16)
            act.activation(rw[:, :, 0, :], wsm[:, C_RW:C_END].rearrange("p (c e) -> p c e", c=HC), ACT.Copy).then_inc(s_rh, 1)
            ffn(0)
            inv_std(1, 0)
            for h in range(2):
                a, z = h * TT // 2, (h + 1) * TT // 2
                if h == 0:
                    highs(1, 0)
                    inv_std(1, 1)
                act.wait_ge(s_kp, h + 1)
                act.activation(kh[:, HALF * h:HALF * (h + 1)], bank[4], ACT.Copy).then_inc(s_kh, 1)
                for g in range(QG):
                    n = QG * h + g
                    act.wait_ge(s_qp, n + 1)
                    if n >= 2:
                        act.wait_ge(s_qs, n - 1)
                    act.activation(qh[:, n % 2, :], bank[5 + g % 2], ACT.Copy, scale=QK_SCALE).then_inc(s_qh, 1)
                    if g % 2 == 0:
                        act.activation(qb[:, 0, :], bank[5], ACT.Copy, scale=kinds[:, 0:1]).then_inc(s_qb, 1)
                    if n == 1:
                        highs(1, 1)
                    if g == 1:
                        act.wait_ge(s_v, h + 1)
                        act.activation(vc[:, a + 1:z + 1, :, 0:D], vf[:, a + 1:z + 1, :, :], ACT.Copy).then_inc(s_vch, 1)
                    if g == 2:
                        act.wait_ge(s_vd, h + 1)
                        act.activation(vdc[:, a:z, :, 0:D], vd[:, a:z], ACT.Copy).then_inc(s_vch, 1)
            for b in range(2):
                first_blocks(1, b)

            def unit(j, k, first=False):
                u = 8 * j + k
                s = k % 2
                if not (first and k == 0):
                    probs_high(u - 1, 1 - s, first and k < 3)
                if k in (1, 5) and not (first and k == 1):
                    inverse_sums(2 * j + (-1 if k == 1 else 0))
                if not (first and k < 2):
                    act.wait_ge(s_pt, u - 1)
                if k % 4 == 0 and not first:
                    act.wait_ge(s_rexp, 2 * j + k // 4 - 1)
                for h in range(QG):
                    lo = (h % 2) * 2 * P
                    if h % 2 == 0:
                        act.wait_ge(s_nm, 2 * u + h // 2 + 1)
                    i = act.activation(prob[:, s, h * P:(h + 1) * P], bank[2 * s + h // 2][:, lo:lo + P],
                                       ACT.Exp, bias=nmax[:, s, h:h + 1], accum_out=psums[:, k // 4, k % 4, h:h + 1])
                i.then_inc(s_exp, 1)
                if k in (2, 6) and not (first and k == 2):
                    heads_high(2 * j + (-1 if k == 2 else 0))

            def probs_high(u, s, first):
                act.wait_ge(s_pt, u + 1)
                if not first:
                    act.wait_ge(s_av, u - 1)
                act.activation(pall[:, s, 0, :], bank[4], ACT.Copy).then_inc(s_pah, 1)

            def inverse_sums(i):
                act.wait_ge(s_rt, i + 1)
                if not (isinstance(i, int) and i == 0):
                    act.wait_ge(s_att, i)
                act.activation(rden[:], bank[7], ACT.Copy).then_inc(s_rden, 1)

            def heads_high(i):
                act.wait_ge(s_att, i + 1)
                if not (isinstance(i, int) and i == 0):
                    act.wait_ge(s_wo, i)
                act.activation(oh[:], att[:], ACT.Copy).then_inc(s_oh, 1)

            for k in range(8):
                unit(0, k, True)
            with act.Fori(1, TT // 2) as j:
                for k in range(8):
                    unit(j, k)
            probs_high(UNITS - 1, 1, False)
            inverse_sums(TT - 1)
            heads_high(TT - 1)
            for h in range(2):
                inv_std(2, h)
                highs(2, h)
            ffn(1)

        @block.tensor
        def _(pe):
            def prep(p, h):
                if p == 0:
                    pe.wait_ge(s_pool, 6)
                for b in (2 * h, 2 * h + 1):
                    pe.wait_ge(s_xn, PAIRS * p + b + 1)
                    for c in range(HC):
                        for t in range(2):
                            at = (2 * c + t) * P
                            i = pe.transpose(bank[b][:, at:at + P], xn[:, 2 * b + t, c * P:(c + 1) * P], ident[:])
                    i.then_inc(s_xt, 1)

            def product(dst, left, right, n_left=None, first=True):
                pairs = [(0, 0), (0, 1), (1, 0)]
                chunks = len(left[0])
                for c in range(chunks):
                    for n, (a, b) in enumerate(pairs):
                        i = pe.matmul(dst, left[a][c], right[b][c], start=first and c == 0 and n == 0,
                                      stop=c == chunks - 1 and n == 2, skip_group_check=not first)
                return i

            def cols(w, at, n):
                return [w[:, at + c * n:at + (c + 1) * n] for c in range(HC)]

            def gate_up(f, j, k, t, r, first=False):
                s = STEPS * f + 4 * j + k
                if first:
                    pe.wait_ge(s_xl, PAIRS * 2 * f + 2 * t + 2)
                pe.wait_ge(s_gul, BLOCKS * f + 2 * j + r + 1)
                if not (first and k < 2):
                    pe.wait_ge(s_h, s - 1)
                for n, sm in ((0, s_g), (1, s_u)):
                    left = [[w[:, r, (2 * n + c) * P:(2 * n + c + 1) * P] for c in range(HC)] for w in (wh, wl)]
                    right = [[v[:, c, HALF * t:HALF * (t + 1)] for c in range(HC)] for v in (xh, xl)]
                    product(bank[4 + 2 * (k % 2) + n], left, right).then_inc(sm, 1)

            def down(f, j, k, t, r):
                pe.wait_ge(s_dwl, BLOCKS * f + 2 * j + r + 1)
                pe.wait_ge(s_hl, STEPS * f + 4 * j + k + 1)
                for tt in range(4):
                    tile_ = 4 * t + tt
                    dst = bank[tile_ // 2][:, (tile_ % 2) * H:(tile_ % 2 + 1) * H]
                    left = [[v[:, k, tt * P:(tt + 1) * P]] for v in (hh, hl)]
                    right = [[w[:, r, GU:WB]] for w in (wh, wl)]
                    i = product(dst, left, right, first=False)
                i.then_inc(s_down, 1)

            def open_sums(banks):
                for b in banks:
                    pe.matmul(bank[b], zeros[:, 0:P], zeros[:], start=True, stop=False, skip_group_check=True)

            def logits():
                for t in range(TT):
                    for n in range(2 * HC):
                        v, c = (xh, xl)[n // HC], n % HC
                        i = pe.matmul(bank[3][:, t * 2 * E:(t + 1) * 2 * E], v[:, c, t * P:(t + 1) * P],
                                      rw[:, c, :, :].rearrange("p a e -> p (a e)"), start=n == 0, stop=n == 2 * HC - 1)
                i.then_inc(s_lp, 1)

            def ffn(f):
                gate_up(f, 0, 0, 0, 0, True)
                prep(2 * f, 1)
                gate_up(f, 0, 1, 0, 1, True)
                if f == 0:
                    pe.wait_ge(s_rl, 1)
                pe.wait_ge(s_xl, PAIRS * (2 * f + 1))
                logits()
                open_sums((0, 1))
                down(f, 0, 0, 0, 0)
                gate_up(f, 0, 2, 1, 0, True)
                down(f, 0, 1, 0, 1)
                gate_up(f, 0, 3, 1, 1, True)
                pe.wait_ge(s_logit, f + 1)
                open_sums((2, 3))
                gate_up(f, 1, 0, 0, 0)
                down(f, 0, 2, 1, 0)
                pe.wait_ge(s_h, STEPS * f + 4)
                pe.wait_ge(s_cw, f + 1)
                pe.transpose(bank[7][0:TT * E, 0:P], r8[:, 6, :], ident[:]).then_inc(s_cwt, 1)
                pe.wait_ge(s_cwc, f + 1)
                gate_up(f, 1, 1, 1, 0)
                down(f, 0, 3, 1, 1)

                def rest_of_pair(j):
                    gate_up(f, j, 2, 0, 1)
                    down(f, j, 0, 0, 0)
                    gate_up(f, j, 3, 1, 1)
                    down(f, j, 1, 1, 0)

                with pe.Fori(1, LAST // 2 - 1) as j:
                    rest_of_pair(j)
                    gate_up(f, j + 1, 0, 0, 0)
                    down(f, j, 2, 0, 1)
                    gate_up(f, j + 1, 1, 1, 0)
                    down(f, j, 3, 1, 1)
                z = LAST // 2
                rest_of_pair(z - 1)
                gate_up(f, z, 0, 0, 0)
                down(f, z - 1, 2, 0, 1)
                gate_up(f, z, 1, 0, 1)
                down(f, z - 1, 3, 1, 1)
                gate_up(f, z, 2, 1, 0)
                down(f, z, 0, 0, 0)
                down(f, z, 1, 0, 1)
                gate_up(f, z, 3, 1, 1)
                down(f, z, 2, 1, 0)
                down(f, z, 3, 1, 1)

            parts = lambda at, n: [cols(w, at, n) for w in (ah, al)]
            xs = lambda a, z: [[v[:, c, a:z] for c in range(HC)] for v in (xh, xl)]

            pe.wait_ge(s_zeros, 1)
            for n in range(WARM):
                pe.matmul(bank[7], zeros[:, 0:P], zeros[:], start=True, stop=True)
            prep(0, 0)
            ffn(0)
            prep(1, 0)
            for h in range(2):
                pe.wait_ge(s_xl, PAIRS + 2 * h + 2)
                if h:
                    pe.wait_ge(s_kl, h)
                product(bank[4], parts(C_WK, P), xs(HALF * h, HALF * (h + 1))).then_inc(s_kp, 1)
                if h:
                    pe.wait_ge(s_v, h)
                for t in range(TT // 2):
                    at = HALF * h + t * P
                    i = product(bank[7][:, t * KV * D:(t + 1) * KV * D], xs(at, at + P), parts(C_WV, KV * D))
                i.then_inc(s_vp, 1)
                for g in range(QG):
                    n = QG * h + g
                    if n >= 2:
                        pe.wait_ge(s_qs, n - 1)
                    left = [[w[:, C_WQ + (c * QG + g) * P:C_WQ + (c * QG + g + 1) * P] for c in range(HC)] for w in (ah, al)]
                    product(bank[5 + g % 2], left, xs(HALF * h, HALF * (h + 1))).then_inc(s_qp, 1)
                    if n == 1:
                        prep(1, 1)

            def scores(j, k, first):
                u, s, g, r = 8 * j + k, k % 2, k % 4, k // 4
                if g == 0:
                    pe.wait_ge(s_ring[r], 48 * (j + 1))
                if not (first and k < 2):
                    pe.wait_ge(s_exp, u - 1)
                rows = slice(32 * g, 32 * (g + 1))
                for h in range(QG):
                    q = qring[rows, r, h * P:(h + 1) * P]
                    lo = (h % 2) * 2 * P
                    b = bank[2 * s + h // 2]
                    if first and r == 0:
                        pe.matmul(b[:, lo:lo + P], negs[rows, 0:P], negs[rows, P:2 * P], start=True, stop=True)
                        a, z = P, 2 * P
                    else:
                        a, z = 0, 2 * P
                    pe.matmul(b[:, lo + a:lo + z], q, khring[rows, r, a:z], start=True, stop=False)
                    i = pe.matmul(b[:, lo + a:lo + z], q, klring[rows, r, a:z], start=False, stop=True)
                    if h % 2:
                        i.then_inc(s_qk[h // 2], 1)

            def turn(u, s, first=False):
                pe.wait_ge(s_exp, u + 1)
                if not first:
                    pe.wait_ge(s_pal, u)
                for h in range(QG):
                    i = pe.transpose(bank[4][:, h * P:(h + 1) * P], prob[:, s, h * P:(h + 1) * P], ident[:])
                i.then_inc(s_pt, 1)

            def values(j, g, s, r, first=False):
                i = 2 * j + r
                pe.wait_ge(s_pal, 4 * i + g + 1)
                if g == 0:
                    pe.wait_ge(s_vr[r], 32 * (j + 1))
                    if not first:
                        pe.wait_ge(s_att, i)
                cs = slice(g * P, (g + 1) * P)
                for w in range(2):
                    o = g == 0 and w == 0
                    pe.matmul(bank[6], vprev[:, r, cs], pall[:, s, w, :], start=o, stop=False, skip_group_check=True)
                for w in range(2):
                    pe.wait_ge(s_pm, 8 * i + 2 * g + w + 1)
                    m = pe.matmul(bank[6], vdiff[:, r, cs], pcur[:, s, w, :], start=False, stop=g == KV - 1 and w == 1, skip_group_check=True)
                m.then_inc(s_av, 1)

            def turn_sums(i):
                pe.wait_ge(s_rexp, i + 1)
                if not (isinstance(i, int) and i == 0):
                    pe.wait_ge(s_rden, i)
                for h in range(QG):
                    m = pe.transpose(bank[7][:, h * P:(h + 1) * P], rexp[:, h, :, :].rearrange("p g r -> p (g r)"), ident[:])
                m.then_inc(s_rt, 1)

            def project(i):
                pe.wait_ge(s_ol, i + 1)
                if not (isinstance(i, int) and i == 0):
                    pe.wait_ge(s_x2, i)
                left = [[v[:, h * P:(h + 1) * P] for h in range(QG)] for v in (oh, ol)]
                right = [[w[:, C_WO + h * H:C_WO + (h + 1) * H] for h in range(QG)] for w in (ah, al)]
                product(bank[5][:, 0:H], left, right).then_inc(s_wo, 1)

            def step(j, k, first=False):
                if k in (5, 1) and not (first and k == 1):
                    turn_sums(2 * j + (0 if k == 5 else -1))
                scores(j, k, first)
                if not (first and k == 0):
                    turn(8 * j + k - 1, (k + 1) % 2, first and k == 1)
                if not (first and k < 2):
                    values(j + (k - 2) // 8, (k - 2) % 4, k % 2, ((k - 2) // 4) % 2, first and k < 6)
                if k in (0, 4) and not (first):
                    project(2 * j + (-1 if k == 4 else -2))

            for k in range(8):
                if k == 1:
                    pe.wait_ge(s_kl, 2)
                    pe.wait_ge(s_qs, 2 * QG)
                step(0, k, True)
            with pe.Fori(1, TT // 2) as j:
                for k in range(8):
                    step(j, k)
            turn(UNITS - 1, 1)
            values(TT // 2 - 1, 2, 0, 1)
            project(TT - 2)
            values(TT // 2 - 1, 3, 1, 1)
            turn_sums(TT - 1)
            project(TT - 1)
            prep(2, 0)
            ffn(1)

        @block.vector
        def _(dve):
            links = [0]

            def link(i):
                links[0] += 1
                i.then_inc(s_dve, 1)
                dve.wait_ge(s_dve, links[0])

            def bn(h):
                for t in range(h * TT // 2, (h + 1) * TT // 2):
                    i = dve.bn_stats(bst[:, t, :], x[:, t, :])
                link(i)

            def variance(h):
                tiles = range(h * TT // 2, (h + 1) * TT // 2)
                ts = slice(tiles[0], tiles[-1] + 1)
                for t in tiles:
                    i = dve.bn_aggr(mv[:, t, :], bst[:, t, :])
                link(i)
                dve.tensor_scalar(ve[:, ts], mv[:, ts, 1], EPS, None, ALU.add).then_inc(s_ve, 1)

            def norm(p, h):
                tiles = range(h * TT // 2, (h + 1) * TT // 2)
                ts = slice(tiles[0], tiles[-1] + 1)
                dve.wait_ge(s_ln, 4 * p + 2 * h + 2)
                link(dve.scalar_tensor_tensor(out=nt[:, 0, ts], in0=ve[:, ts], scalar=-0.5, in1=rs[:, ts],
                                              op0=ALU.mult, op1=ALU.mult))
                link(dve.tensor_tensor(nt[:, 1, ts], nt[:, 0, ts], rs[:, ts], ALU.mult))
                link(dve.scalar_tensor_tensor(out=rs[:, ts], in0=nt[:, 1, ts], scalar=1.5, in1=rs[:, ts],
                                              op0=ALU.add, op1=ALU.mult))
                for b in (2 * h, 2 * h + 1):
                    for t in (2 * b, 2 * b + 1):
                        i = dve.tensor_scalar(xn[:, t, :], x[:, t, :], mv[:, t, 0:1], rs[:, t:t + 1],
                                              ALU.subtract, ALU.mult)
                    i.then_inc(s_xn, 1)

            def lows(p, h):
                for b in (2 * h, 2 * h + 1):
                    dve.wait_ge(s_xh, PAIRS * p + b + 1)
                    cs = slice(2 * P * b, 2 * P * (b + 1))
                    dve.tensor_tensor(xl[:, :, cs], bank[b].rearrange("p (c n) -> p c n", c=HC),
                                      xh[:, :, cs].bitcast(F32), ALU.subtract).then_inc(s_xl, 1)

            def route_scores(f):
                dve.wait_ge(s_lp, f + 1)
                lg = bank[3][:, 0:2 * TT * E].rearrange("p (t a e) -> p t a e", a=2, e=E)
                link(dve.tensor_copy(v3(r8[:, 0, :], E), lg[:, :, 0, :]))
                dve.tensor_tensor(v3(r8[:, 1, :], E), lg[:, :, 1, :], v3(r8[:, 0, :], E), ALU.add).then_inc(s_logit, 1)

            def rank(vals, n, tie, above, equal, dst):
                a = vals.unsqueeze(3).to_broadcast([P, TT, n, n])
                b = vals.unsqueeze(2).to_broadcast([P, TT, n, n])
                v4 = lambda ap: ap.rearrange("p (t i j) -> p t i j", i=n, j=n)
                dve.tensor_tensor(v4(above), b, a, ALU.is_gt)
                link(dve.tensor_tensor(v4(equal), b, a, ALU.is_equal))
                q = equal.rearrange("p (t m) -> p t m", t=TT)
                link(dve.tensor_tensor(q, q, tie[:].rearrange("p i j -> p (i j)").unsqueeze(1).to_broadcast([P, TT, n * n]), ALU.mult))
                link(dve.tensor_tensor(above, above, equal, ALU.add))
                link(dve.tensor_reduce(dst, above.rearrange("p (m j) -> p m j", j=n), AX_X, ALU.add))

            v3 = lambda ap, n: ap.rearrange("p (t e) -> p t e", e=n)
            pairs = r8[:, 3, :].rearrange("p (g two) -> p g two", two=2)

            def route_groups(f):
                dve.wait_ge(s_er, f + 1)
                link(dve.tensor_scalar(r8[:, 1, :], r8[:, 0, :], 1.0, None, ALU.add))
                link(dve.reciprocal(r8[:, 2, :], r8[:, 1, :]))
                if f == 0:
                    dve.wait_ge(s_const, 48)
                    dve.wait_ge(s_pool, 6)
                sfc = v3(r8[:, 3, :], E)
                link(dve.tensor_tensor(sfc, v3(r8[:, 2, :], E), rbias[:].unsqueeze(1).to_broadcast([P, TT, E]), ALU.add))
                link(dve.tensor_tensor(r4[:, 0, :], pairs[:, :, 0], pairs[:, :, 1], ALU.add))

                rank(v3(r4[:, 0, :], NG), NG, tie4, r16[:, 0, :], r16[:, 1, :], r4[:, 1, :])
                link(dve.tensor_scalar(r4[:, 2, :], r4[:, 1, :], 2.0, None, ALU.is_lt))
                gm = r4[:, 2, :].unsqueeze(2).to_broadcast([P, TT * NG, 2])
                link(dve.tensor_tensor(r8[:, 4, :].rearrange("p (g two) -> p g two", two=2), pairs, gm, ALU.mult))

            def route_experts(f):
                big = cwb[:, 3, :].rearrange("p (a n) -> p a n", a=2)
                rank(v3(r8[:, 4, :], E), E, tie8, big[:, 0, :], big[:, 1, :], r8[:, 5, :])
                link(dve.tensor_scalar(r8[:, 5, :], r8[:, 5, :], 2.0, None, ALU.is_lt))
                link(dve.tensor_tensor(r8[:, 5, :], r8[:, 5, :], r8[:, 2, :], ALU.mult))
                link(dve.tensor_reduce(r4[:, 3, 0:TT], v3(r8[:, 5, :], E), AX_X, ALU.add))
                link(dve.tensor_scalar(r4[:, 3, 0:TT], r4[:, 3, 0:TT], 1e-20, None, ALU.add))
                link(dve.reciprocal(r4[:, 3, TT:2 * TT], r4[:, 3, 0:TT]))
                link(dve.tensor_scalar(r4[:, 3, TT:2 * TT], r4[:, 3, TT:2 * TT], SCALE, None, ALU.mult))
                cw = r8[:, 6, :].rearrange("p (e t) -> p t e", e=E)
                dve.tensor_tensor(cw, v3(r8[:, 5, :], E), r4[:, 3, TT:2 * TT].unsqueeze(2).to_broadcast([P, TT, E]),
                                  ALU.mult).then_inc(s_cw, 1)


            def half_step(f, j, k, row=None, meanwhile=None):
                s = STEPS * f + 4 * j + k
                h = act_h[:, k, :]
                dve.wait_ge(s_silu, s + 1)
                if row is not None:
                    n = s + 1 - 4 * (f + 1)
                    dve.tensor_tensor(h, h, row, ALU.mult).then_inc(s_cwm, 1)
                    dve.wait_ge(s_cwm, n)
                dve.wait_ge(s_u, s + 1)
                dve.tensor_tensor(h, bank[5 + 2 * (k % 2)], h, ALU.mult).then_inc(s_h, 1)
                if meanwhile:
                    meanwhile()
                dve.wait_ge(s_hh, s + 1)
                dve.tensor_tensor(hl[:, k, :], h, hh[:, k, :].bitcast(F32), ALU.subtract).then_inc(s_hl, 1)

            def finish(f, h):
                dve.wait_ge(s_down, STEPS * (f + 1) - 2 + 2 * h)
                for b in (2 * h, 2 * h + 1):
                    xs = x[:, 2 * b:2 * b + 2, :].rearrange("p t h -> p (t h)")
                    i = dve.scalar_tensor_tensor(out=xs, in0=bank[b], scalar=0.5, in1=xs, op0=ALU.mult, op1=ALU.add)
                    i.then_inc(s_fin, 1)

            def ffn(f):
                def row_of(b, t):
                    if isinstance(b, int):
                        b = max(b - SH_BLOCKS + 1, 0)
                        return cwb[:, b, HALF * t:HALF * (t + 1)]
                    return cwb[:, bass.ds(b - SH_BLOCKS + 1, 1), HALF * t:HALF * (t + 1)].rearrange("p a n -> p (a n)")

                def pair(j):
                    for k in range(4):
                        half_step(f, j, k, row_of(2 * j + k // 2, k % 2))

                half_step(f, 0, 0)
                half_step(f, 0, 1)
                route_scores(f)
                route_groups(f)
                half_step(f, 0, 2)
                route_experts(f)
                half_step(f, 0, 3)
                dve.wait_ge(s_ones, f + 1)
                half_step(f, 1, 0, row_of(2, 0))
                half_step(f, 1, 1, row_of(2, 1))
                dve.wait_ge(s_cwb[0], 16 * N_CWB[0] * (f + 1))
                half_step(f, 1, 2, row_of(3, 0))
                half_step(f, 1, 3, row_of(3, 1))
                dve.wait_ge(s_cwb[1], 16 * N_CWB[1] * (f + 1))
                with dve.Fori(2, 4) as j:
                    pair(j)
                dve.wait_ge(s_cwb[2], 16 * N_CWB[2] * (f + 1))
                with dve.Fori(4, LAST // 2) as j:
                    pair(j)
                z = LAST // 2
                half_step(f, z, 0, row_of(LAST, 0))
                half_step(f, z, 1, row_of(LAST + 1, 0))
                half_step(f, z, 2, row_of(LAST, 1))
                finish(f, 0)
                if f == 0:
                    dve.wait_ge(s_fin, 2)
                    bn(0)
                half_step(f, z, 3, row_of(LAST + 1, 1), (lambda: variance(0)) if f == 0 else None)
                if f == 0:
                    norm(1, 0)
                finish(f, 1)

            dve.wait_ge(s_x[0], 16)
            bn(0)
            variance(0)
            norm(0, 0)
            dve.wait_ge(s_x[1], 16)
            bn(1)
            variance(1)
            lows(0, 0)
            norm(0, 1)
            lows(0, 1)
            ffn(0)

            def keys_low(h):
                cs = slice(HALF * h, HALF * (h + 1))
                dve.wait_ge(s_kh, h + 1)
                dve.tensor_tensor(kl[:, cs], bank[4], kh[:, cs].bitcast(F32), ALU.subtract).then_inc(s_kl, 1)

            def take_values(h):
                dve.wait_ge(s_vp, h + 1)
                dve.tensor_copy(vf[:, 1 + h * TT // 2:1 + (h + 1) * TT // 2, :, :],
                                bank[7][:, 0:TT // 2 * KV * D].rearrange("p (t g d) -> p t g d", t=TT // 2, g=KV)).then_inc(s_v, 1)

            def both_parts(h):
                for g in range(QG):
                    n = QG * h + g
                    dve.wait_ge(s_qh, n + 1)
                    if g % 2:
                        dve.tensor_scalar(qb[:, 1, :], bank[6], kinds[:, 0:1], None, ALU.mult).then_inc(s_qd, 1)
                        dve.wait_ge(s_qd, n // 2 + 1)
                    else:
                        dve.wait_ge(s_qb, n // 2 + 1)
                    dve.scalar_tensor_tensor(out=qs[:, g, HALF * h:HALF * (h + 1)],
                                             in0=qh[:, n % 2, :].bitcast(F32), scalar=kinds[:, 1:2], in1=qb[:, n % 2, :],
                                             op0=ALU.mult, op1=ALU.add).then_inc(s_qs, 1)
                    if n == 1:
                        lows(1, 1)

            lows(1, 0)
            dve.wait_ge(s_fin, PAIRS)
            bn(1)
            variance(1)
            keys_low(0)
            norm(1, 1)
            take_values(0)
            both_parts(0)
            keys_low(1)
            take_values(1)
            both_parts(1)

            def pick_max(j, k):
                u, s = 8 * j + k, k % 2
                for b in range(2):
                    v = bank[2 * s + b].rearrange("p (h w k) -> p h w k", h=2, w=2)
                    dve.wait_ge(s_qk[b], u + 1)
                    dve.memset(idle[:, 2 * s + b:2 * s + b + 1], 0.0)
                    dve.copy_predicated(v[:, :, 0, :], sel_q[:].bitcast(I32), v[:, :, 1, :]).then_inc(s_sel, 1)
                for b in range(2):
                    v = bank[2 * s + b].rearrange("p (h w k) -> p h w k", h=2, w=2)
                    dve.wait_ge(s_sel, 2 * u + b + 1)
                    dve.tensor_reduce(nmax[:, s, 2 * b:2 * b + 2], v[:, :, 0, :], AX_X, ALU.max, negate=True).then_inc(s_nm, 1)

            def probs_low(u, s):
                dve.wait_ge(s_pah, u + 1)
                dve.tensor_tensor(pall[:, s, 1, :], bank[4], pall[:, s, 0, :].bitcast(F32), ALU.subtract).then_inc(s_pal, 1)

            def invert_sums(i, k):
                dve.wait_ge(s_exp, 4 * i + 4)
                dve.reciprocal(rsums[:], psums[:, k, :, :]).then_inc(s_rd, 1)
                if not (isinstance(i, int) and i == 0):
                    dve.wait_ge(s_rt, i)
                dve.wait_ge(s_rd, i + 1)
                dve.tensor_copy(rexp[:], rsums[:].rearrange("p g h -> p h g").unsqueeze(3).to_broadcast([P, QG, KV, GR]))\
                   .then_inc(s_rexp, 1)

            def normalise(i):
                dve.wait_ge(s_av, 4 * i + 4)
                if not (isinstance(i, int) and i == 0):
                    dve.wait_ge(s_ol, i)
                dve.wait_ge(s_rden, i + 1)
                dve.tensor_tensor(att[:], bank[6], rden[:], ALU.mult).then_inc(s_att, 1)

            def add_heads(i):
                dve.wait_ge(s_wo, i + 1)
                dve.wait_ge(s_xb, i + 1)
                xs = x[:, i, :] if isinstance(i, int) else x[:, bass.ds(i, 1), :].rearrange("p a n -> p (a n)")
                dve.tensor_tensor(xs, bank[5][:, 0:H], xs, ALU.add).then_inc(s_x2, 1)

            def step(j, k, first=False):
                pick_max(j, k)
                if not (first and k == 0):
                    probs_low(8 * j + k - 1, (k + 1) % 2)
                if k == 4:
                    invert_sums(2 * j, 0)
                if k == 0 and not first:
                    invert_sums(2 * j - 1, 1)
                if k == 5:
                    normalise(2 * j)
                if k == 1 and not first:
                    normalise(2 * j - 1)
                if k in (0, 4) and not first:
                    add_heads(2 * j + (-1 if k == 4 else -2))

            dve.wait_ge(s_pads, 2)
            for k in range(8):
                step(0, k, True)
            with dve.Fori(1, TT // 2) as j:
                for k in range(8):
                    step(j, k)
            probs_low(UNITS - 1, 1)
            invert_sums(TT - 1, 1)
            add_heads(TT - 2)
            normalise(TT - 1)
            add_heads(TT - 1)
            dve.wait_ge(s_x2, TT)
            dve.memset(cwb[:, 0, :], 1.0).then_inc(s_ones, 1)
            bn(0)
            variance(0)
            norm(2, 0)
            bn(1)
            variance(1)
            lows(2, 0)
            norm(2, 1)
            lows(2, 1)
            ffn(1)


def _lay_out(np, a):
    def hidden_rows(shared, routed):
        pad = np.zeros((SH_BLOCKS * P - I_SHARED, H), np.float32)
        rows = np.concatenate([shared, pad, routed.reshape(E * I_MOE, H)])
        return rows.reshape(BLOCKS, P, H)

    gate = hidden_rows(a["L0_ffn_shared_gate_w"], a["L0_ffn_gate_w"]).reshape(BLOCKS, P, HC, P)
    up = hidden_rows(a["L0_ffn_shared_up_w"], a["L0_ffn_up_w"]).reshape(BLOCKS, P, HC, P)
    down = hidden_rows(a["L0_ffn_shared_down_w"].T, a["L0_ffn_down_w"].transpose(0, 2, 1))
    to_cols = lambda w: w.transpose(3, 0, 2, 1).reshape(P, BLOCKS, HC * P)
    blocks = np.concatenate([to_cols(gate), to_cols(up), down.transpose(1, 0, 2)], axis=2)

    wq = a["L0_attn_Wq"].reshape(HC, P, KV, QG, 1, D)
    wq = np.concatenate([wq, wq], axis=4).transpose(1, 0, 3, 2, 4, 5).reshape(P, HC * QG * P)
    wk = a["L0_attn_Wk"].reshape(HC, P, KV, 1, D)
    wk = np.concatenate([wk, wk], axis=3).transpose(1, 0, 2, 3, 4).reshape(P, HC * P)
    wv = a["L0_attn_Wv"].reshape(HC, P, KV * D).transpose(1, 0, 2).reshape(P, HC * KV * D)
    wo = a["L0_attn_Wo"].reshape(KV, QG, 1, D, H)
    wo = np.concatenate([wo, wo], axis=2).transpose(0, 2, 3, 1, 4).reshape(P, QG * H)
    rw = a["L0_ffn_router_weight"].T.reshape(HC, P, E).transpose(1, 0, 2).reshape(P, HC * E)
    small = np.concatenate([wq, wk, wv, wo, rw], axis=1)

    kinds = np.zeros((P // (2 * D), 2, D, 2), np.float32)
    kinds[:, 0, :, 1] = 1.0
    kinds[:, 1, :, 0] = QK_SCALE
    kinds[:, 1, :, 1] = -1.0
    return {
        "x_in": a["L0_attn_x"], "w_blocks": blocks, "w_small": small, "row_kind": kinds.reshape(P, 2),
        "router_bias": a["L0_ffn_e_score_correction_bias"], "out_bias": a["L0_attn_bo"],
    }


def kernel(**inputs):
    import numpy as np
    import concourse.bacc as bacc
    from concourse import mybir as _mybir
    from concourse.bass_utils import run_bass_kernel_spmd as run

    nc = bacc.Bacc("TRN2", target_bir_lowering=False, num_devices=1)
    arrays = {k: np.ascontiguousarray(v) for k, v in _lay_out(np, {k: np.asarray(v) for k, v in inputs.items()}).items()}
    args = [nc.dram_tensor(k, v.shape, _mybir.dt.from_np(v.dtype), kind="ExternalInput").ap() for k, v in arrays.items()]
    out = nc.dram_tensor("out_dram", (1, T, H), F32, kind="ExternalOutput").ap()
    macaron_kernel(nc, *args, out)
    return run(nc, [arrays], core_ids=[0]).results[0]["out_dram"]
```

```python
from contextlib import ExitStack

import concourse.bass as bass
from concourse import mybir

F32 = mybir.dt.float32
F32R = mybir.dt.float32r
BF16 = mybir.dt.bfloat16
I32 = mybir.dt.int32
ALU = mybir.AluOpType
ACT = mybir.ActivationFunctionType
AX_X = mybir.AxisListType.X

P = 128
T = 1024
TT = T // P
H = 256
HC = H // P
E = 8
NG = 4
I_MOE = 176
I_SHARED = 352
SH_BLOCKS = -(-I_SHARED // P)
RT_BLOCKS = E * I_MOE // P
BLOCKS = SH_BLOCKS + RT_BLOCKS
HALF = 512
STEPS = 2 * BLOCKS
WARM = 18
LAST = BLOCKS - 2
GU = 4 * P
WB = GU + H
SCALE = 2.5
EPS = 1e-5

HEADS = 16
KV = 4
QG = HEADS // KV
D = 16
UNITS = TT * KV
QK_SCALE = 0.25
NEG = -1e30
GR = 2 * D

C_WQ = 0
C_WK = C_WQ + HC * QG * P
C_WO = C_WK + HC * P
C_WV = C_WO + QG * H
C_RW = C_WV + HC * KV * D
C_END = C_RW + HC * E


def macaron_kernel(nc, x_in, w_blocks, w_small, row_kind, router_bias, out_bias, out):
    with ExitStack() as ctx:
        def sb(name, shape, dt=F32, stack=ctx):
            return stack.enter_context(nc.sbuf_tensor(name, shape, dt))

        def sem(name):
            return ctx.enter_context(nc.semaphore(name))

        psum = ctx.enter_context(nc.psum_tensor("psum", [P, 8, 512], F32))
        bank = [psum[:, i, :] for i in range(8)]

        x = sb("x", [P, TT, H])
        xh = sb("xh", [P, HC, T], F32R)
        xl = sb("xl", [P, HC, T], F32R)
        wraw = sb("wraw", [P, BLOCKS, WB])
        wh = sb("wh", [P, 2, WB], F32R)
        wl = sb("wl", [P, 2, WB], F32R)
        ah = sb("ah", [P, C_WV], F32R)
        al = sb("al", [P, C_WV], F32R)
        rw = sb("rw", [P, HC, P], F32R)
        wv = sb("wv", [P, HC, 2, KV * D], F32R)
        ident = sb("ident", [P, P])
        zeros = sb("zeros", [P, 512], BF16)
        negs = sb("negs", [P, 2 * P], BF16)
        sel_q = sb("sel_q", [P, 2, P])
        vprev = sb("vprev", [P, 2, KV * (P + GR)], F32R)
        vdiff = sb("vdiff", [P, 2, KV * (P + GR)], F32R)
        kinds = sb("kinds", [P, 2])
        rbias = sb("rbias", [P, E])
        obias = sb("obias", [P, H])
        bst = sb("bst", [P, TT, 6])
        mv = sb("mv", [P, TT, 2])
        ve = sb("ve", [P, TT])
        lnv = sb("lnv", [P, TT])
        rs = sb("rs", [P, TT])
        nt = sb("nt", [P, 2, TT])
        r8 = sb("r8", [P, 8, TT * E])
        r4 = sb("r4", [P, 4, TT * NG])
        r16 = sb("r16", [P, 2, TT * NG * NG])
        tie4 = sb("tie4", [P, NG, NG])
        tie8 = sb("tie8", [P, E, E])
        cwt = sb("cwt", [TT * E, P])
        with ExitStack() as ffn_stack:
            cwb = sb("cwb", [P, RT_BLOCKS, T], F32, ffn_stack)
            act_h = sb("act_h", [P, 4, HALF], F32, ffn_stack)
            hh = sb("hh", [P, 4, HALF], F32R, ffn_stack)
            hl = sb("hl", [P, 4, HALF], F32R, ffn_stack)
        with ExitStack() as attn_stack:
            vf = sb("vf", [P, TT + 1, KV, D], F32, attn_stack)
            vd = sb("vd", [P, TT, KV, D], F32, attn_stack)
            vc = sb("vc", [P, TT + 1, KV, GR], F32R, attn_stack)
            vdc = sb("vdc", [P, TT, KV, GR], F32R, attn_stack)
            kh = sb("kh", [P, T], F32R, attn_stack)
            kl = sb("kl", [P, T], F32R, attn_stack)
            qs = sb("qs", [P, QG, T], F32R, attn_stack)
            keys = sb("keys", [P, 2, T], F32R, attn_stack)
            qring = sb("qring", [P, 2, 2, QG * P], F32R, attn_stack)
            kring = sb("kring", [P, 2, 2, 2 * P], F32R, attn_stack)
            nmax = sb("nmax", [P, 2, QG], F32, attn_stack)
            prob = sb("prob", [P, 2, QG * P], F32, attn_stack)
            pall = sb("pall", [P, 2, 2, QG * P], F32R, attn_stack)
            pcur = sb("pcur", [P, 2, 2, QG * P], F32R, attn_stack)
            qh = pcur[:, 0, :, :]
            qb = prob
            idle_p = sb("idle_p", [P, 4], F32, attn_stack)
            idle = sb("idle", [P, 4], F32, attn_stack)
            psums = sb("psums", [P, 2, KV, QG], F32, attn_stack)
            rsums = sb("rsums", [P, KV, QG], F32, attn_stack)
            rexp = sb("rexp", [P, QG, KV, GR], F32, attn_stack)
            rden = sb("rden", [P, QG * P], F32, attn_stack)
            att = sb("att", [P, QG * P], F32, attn_stack)
            oh = sb("oh", [P, QG * P], F32R, attn_stack)
            ol = sb("ol", [P, QG * P], F32R, attn_stack)
            xn2 = sb("xn2", [P, 2, 2, H], F32, attn_stack)
        wsm = cwb[:, RT_BLOCKS - 3:RT_BLOCKS, :].rearrange("p a b -> p (a b)")
        xn = act_h[:, :, :].rearrange("p a (b n) -> p (a b) n", n=H)
        lgt = cwb[0:2 * E, 4, :]
        cw_dram = nc.dram_tensor("cw_dram", (TT * E, P), F32, kind="Internal").ap()

        s_x = [sem(f"s_x{k}") for k in range(2)]
        s_w = [sem(f"s_w{k}") for k in range(3)]
        s_small = sem("s_small")
        s_router = sem("s_router")
        s_rz = sem("s_rz")
        s_rh = sem("s_rh")
        s_rl = sem("s_rl")
        s_const = sem("s_const")
        s_pool = sem("s_pool")
        s_zeros = sem("s_zeros")
        s_ah = sem("s_ah")
        s_al = sem("s_al")
        s_dve = sem("s_dve")
        s_ve = sem("s_ve")
        s_ln = sem("s_ln")
        s_xn = sem("s_xn")
        s_xt = sem("s_xt")
        s_xh = sem("s_xh")
        s_xl = sem("s_xl")
        s_lp = sem("s_lp")
        s_lc = sem("s_lc")
        s_lt = sem("s_lt")
        s_logit = sem("s_logit")
        s_er = sem("s_er")
        s_cw = sem("s_cw")
        s_cwt = sem("s_cwt")
        s_cwc = sem("s_cwc")
        s_cwd = sem("s_cwd")
        s_cwb = [sem(f"s_cwb{k}") for k in range(3)]
        s_guh = sem("s_guh")
        s_gul = sem("s_gul")
        s_dwh = sem("s_dwh")
        s_dwl = sem("s_dwl")
        s_g = sem("s_g")
        s_u = sem("s_u")
        s_silu = sem("s_silu")
        s_cwm = sem("s_cwm")
        s_h = sem("s_h")
        s_hh = sem("s_hh")
        s_hl = sem("s_hl")
        s_down = sem("s_down")
        s_fin = sem("s_fin")
        s_xb = sem("s_xb")
        s_kp = sem("s_kp")
        s_kh = sem("s_kh")
        s_kl = sem("s_kl")
        s_vp = sem("s_vp")
        s_v = sem("s_v")
        s_qp = sem("s_qp")
        s_qh = sem("s_qh")
        s_qb = sem("s_qb")
        s_qs = sem("s_qs")
        s_pads = sem("s_pads")
        s_keys = [sem(f"s_keys{k}") for k in range(2)]
        s_tkeys = [sem(f"s_tkeys{k}") for k in range(2)]
        s_queries = [[sem(f"s_queries{k}{c}") for c in range(2)] for k in range(2)]
        s_qk = [sem(f"s_qk{k}") for k in range(2)]
        s_sel = sem("s_sel")
        s_nm = sem("s_nm")
        s_exp = [sem(f"s_exp{k}") for k in range(2)]
        s_pt = [sem(f"s_pt{k}") for k in range(2)]
        s_pah = [sem(f"s_pah{k}") for k in range(2)]
        s_pal = [sem(f"s_pal{k}") for k in range(2)]
        s_pm = sem("s_pm")
        s_vz = sem("s_vz")
        s_vd = sem("s_vd")
        s_vch = sem("s_vch")
        s_vcl = sem("s_vcl")
        s_vr = [sem(f"s_vr{k}") for k in range(2)]
        s_av = sem("s_av")
        s_rd = sem("s_rd")
        s_rexp = sem("s_rexp")
        s_rt = sem("s_rt")
        s_rden = sem("s_rden")
        s_att = sem("s_att")
        s_oh = sem("s_oh")
        s_ol = sem("s_ol")
        s_wo = sem("s_wo")
        s_x2 = sem("s_x2")
        s_out = sem("s_out")
        PAIRS = TT // 2
        LASTJ = TT // 2 - 1

        def half_tiles(h):
            return slice(h * TT // 2, (h + 1) * TT // 2)

        def pair_tiles(b):
            return slice(2 * b, 2 * b + 2)

        def turn_bank(b):
            return bank[(5, 5, 0, 1)[b]]

        block = ctx.enter_context(nc.Block())

        def small_part(k):
            return slice(k * C_WV // 3, (k + 1) * C_WV // 3)

        def block_cols(b, a, z):
            if isinstance(b, int):
                return wraw[:, b, a:z]
            return wraw[:, bass.ds(b, 1), a:z].rearrange("p a n -> p (a n)")

        def diagonal(v, k):
            return v[:, k, :].rearrange("p (g n) -> p g n", g=KV)[:, :, 0:GR]

        def expert_runs(b):
            at, runs = 0, []
            while at < P:
                e = (b * P + at) // I_MOE
                n = min(P - at, (e + 1) * I_MOE - b * P - at)
                runs.append((at, n, e))
                at += n
            return runs

        def stage_of(b):
            return (b > 0) + (b > 4)

        N_CWB = [sum(len(expert_runs(b)) for b in range(RT_BLOCKS) if stage_of(b) == k) for k in range(3)]

        @block.sync
        def _(sp):
            x_tiles = x_in.rearrange("a (t p) h -> p (a t) h", p=P)
            sp.dma_start(x[:, 0:4, :], x_tiles[:, 0:4, :]).then_inc(s_x[0], 16)
            sp.dma_start(wraw[:, 0, :], w_blocks[:, 0, :]).then_inc(s_w[0], 16)
            sp.dma_start(x[:, 4:8, :], x_tiles[:, 4:8, :]).then_inc(s_x[1], 16)
            sp.dma_start(wraw[:, 1, :], w_blocks[:, 1, :]).then_inc(s_w[1], 16)
            sp.dma_start(wsm[:, C_RW:C_END], w_small[:, C_RW:C_END]).then_inc(s_router, 16)
            sp.dma_start(kinds[:], row_kind).then_inc(s_const, 16)
            sp.dma_start(rbias[:], router_bias.partition_broadcast(P)).then_inc(s_const, 16)
            sp.dma_start(obias[:], out_bias.partition_broadcast(P)).then_inc(s_const, 16)
            sp.dma_start(wsm[:, 0:C_RW], w_small[:, 0:C_RW]).then_inc(s_small, 16)
            for b in range(2, BLOCKS, 3):
                sp.dma_start(wraw[:, b:b + 3, :], w_blocks[:, b:b + 3, :]).then_inc(s_w[2], 16)

            def combine_weights(f):
                sp.wait_ge(s_cwc, f + 1)
                sp.dma_start(cw_dram, cwt[:]).then_inc(s_cwd, 16)
                sp.wait_ge(s_cwd, 16 * (f + 1))
                rows = cw_dram.rearrange("(e t) p -> e (t p)", e=E)
                for b in range(RT_BLOCKS):
                    if f == 0 and b == RT_BLOCKS - 3:
                        sp.wait_ge(s_al, 4)
                    for at, n, e in expert_runs(b):
                        sp.dma_start(cwb[at:at + n, b, :], rows[e, :].partition_broadcast(n)).then_inc(s_cwb[stage_of(b)], 16)
            def place_keys(h):
                sp.wait_ge(s_kl, h + 1)
                cs = slice(HALF * h, HALF * (h + 1))
                for d in range(2):
                    for c in range(2):
                        for g in range(2):
                            to, fr = 2 * GR * g + GR * d, 2 * GR * c + GR * g
                            sp.dma_start(keys[to:to + GR, c, cs].bitcast(F32), (kh, kl)[d][fr:fr + GR, cs].bitcast(F32))\
                              .then_inc(s_keys[h], 16)

            def tile_keys(i, k):
                alone = isinstance(i, int) and i == 0
                w = slice(0, P) if alone else bass.ds(i * P - P, 2 * P)
                sp.dma_start(kring[:, k, :, (P if alone else 0):2 * P].bitcast(F32), keys[:, :, w].bitcast(F32))\
                  .then_inc(s_tkeys[k], 16)

            def tile_queries(i, k):
                for c in range(2):
                    for d in range(2):
                        for g in range(2):
                            to, fr = 2 * GR * g + GR * d, 2 * GR * c + GR * g
                            sp.dma_start(qring[to:to + GR, k, c, :].rearrange("p (h q) -> p h q", h=QG).bitcast(F32),
                                         qs[fr:fr + GR, :, bass.ds(i * P, P)].bitcast(F32)).then_inc(s_queries[k][c], 16)

            def tile_values(i, k):
                for dst, src in ((vprev, vc), (vdiff, vdc)):
                    v = src[:, bass.ds(i, 1), :, :].rearrange("p a g w -> p (a g) w")
                    sp.dma_start(diagonal(dst, k).bitcast(F32), v.bitcast(F32)).then_inc(s_vr[k], 16)

            combine_weights(0)
            place_keys(0)
            sp.wait_ge(s_keys[0], 8 * 16)
            for i in range(2):
                tile_keys(i, i)
            sp.wait_ge(s_qs, QG)
            tile_queries(0, 0)
            sp.wait_ge(s_vcl, 2)
            tile_values(0, 0)
            tile_queries(1, 1)
            tile_values(1, 1)
            place_keys(1)
            sp.wait_ge(s_keys[1], 8 * 16)
            with sp.Fori(1, TT // 2) as j:
                for k in range(2):
                    i = 2 * j + k
                    sp.wait_ge(s_qs, 2 * QG)
                    sp.wait_ge(s_qk[1], 4 * i - 4)
                    tile_keys(i, k)
                    tile_queries(i, k)
                    sp.wait_ge(s_vcl, 4)
                    sp.wait_ge(s_av, 4 * i - 4)
                    tile_values(i, k)
            combine_weights(1)
            out_tiles = out.rearrange("a (t p) h -> p (a t) h", p=P)
            for b in range(PAIRS):
                sp.wait_ge(s_fin, PAIRS + b + 1)
                sp.dma_start(out_tiles[:, 2 * b:2 * b + 2, :], x[:, 2 * b:2 * b + 2, :]).then_inc(s_out, 16)
            sp.wait_ge(s_out, 16 * PAIRS)

        @block.gpsimd
        def _(pool):
            pool.memset(ident[:], 0.0).then_inc(s_pool, 1)
            pool.memset(rw[:].bitcast(F32), 0.0).then_inc(s_rz, 1)
            pool.memset(zeros[:], 0.0).then_inc(s_zeros, 1)
            pool.memset(negs[:, 0:P], 1.0 / (2 * GR))
            pool.memset(negs[:, P:2 * P], NEG)
            pool.memset(tie4[:], 1.0).then_inc(s_pool, 1)
            pool.memset(tie8[:], 1.0).then_inc(s_pool, 1)
            pool.wait_ge(s_pool, 3)
            pool.affine_select(out=ident[:], in_=ident[:], compare_op=ALU.not_equal, fill=1.0, base=0,
                               pattern=[[-1, P]], channel_multiplier=1).then_inc(s_pool, 1)
            pool.affine_select(out=tie4[:], in_=tie4[:], compare_op=ALU.is_gt, fill=0.0, base=0,
                               pattern=[[1, NG], [-1, NG]], channel_multiplier=0).then_inc(s_pool, 1)
            pool.affine_select(out=tie8[:], in_=tie8[:], compare_op=ALU.is_gt, fill=0.0, base=0,
                               pattern=[[1, E], [-1, E]], channel_multiplier=0).then_inc(s_pool, 1)
            pool.memset(sel_q[:], 1.0)
            pool.memset(vprev[:].bitcast(F32), 0.0)
            pool.memset(vdiff[:].bitcast(F32), 0.0).then_inc(s_pads, 1)
            pool.wait_ge(s_pads, 1)
            pool.affine_select(out=sel_q[:], in_=sel_q[:], compare_op=ALU.is_ge, fill=0.0, base=0,
                               pattern=[[0, 2], [-1, P]], channel_multiplier=1).then_inc(s_pads, 1)

            def low_gate_up(b, r, n):
                pool.wait_ge(s_guh, n)
                pool.tensor_tensor(wl[:, r, 0:GU], block_cols(b, 0, GU), wh[:, r, 0:GU].bitcast(F32),
                                   ALU.subtract).then_inc(s_gul, 1)

            def low_down(b, r, n):
                pool.wait_ge(s_dwh, n)
                pool.tensor_tensor(wl[:, r, GU:WB], block_cols(b, GU, WB), wh[:, r, GU:WB].bitcast(F32),
                                   ALU.subtract).then_inc(s_dwl, 1)

            def first_low_parts(f):
                for b in range(2):
                    low_gate_up(b, b, BLOCKS * f + b + 1)
                    low_down(b, b, BLOCKS * f + b + 1)

            def low_parts(f):
                n = BLOCKS * f + 1
                low_gate_up(2, 0, n + 2)
                if f == 0:
                    small_low(2)
                    pool.wait_ge(s_ah, 4)
                    pool.tensor_tensor(wv[:, :, 1, :], wsm[:, C_WV:C_RW].rearrange("p (c n) -> p c n", c=HC),
                                       wv[:, :, 0, :].bitcast(F32), ALU.subtract).then_inc(s_al, 1)
                with pool.Fori(1, LAST // 2) as j:
                    for k in range(2):
                        low_gate_up(2 * j + k + 1, 1 - k, n + 2 * j + k + 1)
                        low_down(2 * j + k, k, n + 2 * j + k)
                low_gate_up(LAST + 1, 1, n + LAST + 1)
                low_down(LAST, 0, n + LAST)
                low_down(LAST + 1, 1, n + LAST + 1)

            def small_low(k):
                w = small_part(k)
                pool.wait_ge(s_ah, k + 1)
                pool.tensor_tensor(al[:, w], wsm[:, w], ah[:, w].bitcast(F32), ALU.subtract).then_inc(s_al, 1)

            first_low_parts(0)
            pool.wait_ge(s_rh, 1)
            pool.tensor_tensor(rw[:, :, E:2 * E], wsm[:, C_RW:C_END].rearrange("p (c e) -> p c e", c=HC),
                               rw[:, :, 0:E].bitcast(F32), ALU.subtract).then_inc(s_rl, 1)
            small_low(0)
            small_low(1)
            low_parts(0)

            pool.memset(vf[:, 0, :, :], 0.0)
            pool.memset(vc[:, 0, :, :].bitcast(F32), 0.0).then_inc(s_vz, 1)
            pool.wait_ge(s_vz, 1)
            for h in range(2):
                a, z = h * TT // 2, (h + 1) * TT // 2
                pool.wait_ge(s_v, h + 1)
                pool.tensor_tensor(vd[:, a:z], vf[:, a + 1:z + 1, :, :], vf[:, a:z, :, :], ALU.subtract).then_inc(s_vd, 1)
                pool.wait_ge(s_vch, 2 * h + 1)
                pool.tensor_tensor(vc[:, a + 1:z + 1, :, D:GR], vf[:, a + 1:z + 1, :, :],
                                   vc[:, a + 1:z + 1, :, 0:D].bitcast(F32), ALU.subtract).then_inc(s_vcl, 1)
                pool.wait_ge(s_vch, 2 * h + 2)
                pool.tensor_tensor(vdc[:, a:z, :, D:GR], vd[:, a:z], vdc[:, a:z, :, 0:D].bitcast(F32),
                                   ALU.subtract).then_inc(s_vcl, 1)
            pool.wait_ge(s_const, 48)
            pool.wait_ge(s_xl, 2 * PAIRS)
            for t in range(TT):
                pool.tensor_tensor(x[:, t, :], x[:, t, :], obias[:], ALU.add).then_inc(s_xb, 1)

            def own_tile(j, k, first=False):
                u, s = 8 * j + k, k % 2
                if not (first and k < 2):
                    pool.wait_ge(s_av, u - 1)
                for w, there in ((0, s_pah[1]), (1, s_pal[1])):
                    pool.wait_ge(there, u + 1)
                    pool.tensor_tensor(idle_p[:, 2 * s + w:2 * s + w + 1], kinds[:, 0:1], kinds[:, 1:2], ALU.add)
                    pool.affine_select(out=pcur[:, s, w, :].rearrange("p (h q) -> p h q", h=QG),
                                       in_=pall[:, s, w, :].rearrange("p (h q) -> p h q", h=QG),
                                       compare_op=ALU.is_ge, fill=0.0, base=0,
                                       pattern=[[0, QG], [1, P]], channel_multiplier=-1).then_inc(s_pm, 1)

            def heads_low(i):
                pool.wait_ge(s_oh, i + 1)
                if not (isinstance(i, int) and i == 0):
                    pool.wait_ge(s_wo, i)
                pool.tensor_tensor(ol[:], att[:], oh[:].bitcast(F32), ALU.subtract).then_inc(s_ol, 1)

            def unit(j, k, first=False):
                own_tile(j, k, first)
                if k == 6:
                    heads_low(2 * j)
                if k == 2 and not first:
                    heads_low(2 * j - 1)

            for k in range(8):
                unit(0, k, True)
            with pool.Fori(1, LASTJ) as j:
                for k in range(8):
                    unit(j, k)
            for k in range(8):
                unit(LASTJ, k)
                if k in (0, 2):
                    low_gate_up(k // 2, k // 2, BLOCKS + k // 2 + 1)
                if k in (3, 6):
                    low_down(k // 3 - 1, k // 3 - 1, BLOCKS + k // 3)
            low_parts(1)

        @block.scalar
        def _(act):
            def inv_std(n, ts):
                act.wait_ge(s_ve, n + 1)
                act.activation(lnv[:, ts], ve[:, ts], ACT.Ln).then_inc(s_ln, 1)
                act.wait_ge(s_ln, 2 * n + 1)
                act.activation(rs[:, ts], lnv[:, ts], ACT.Exp, scale=-0.5).then_inc(s_ln, 1)

            def highs(p, h):
                for b in (2 * h, 2 * h + 1):
                    act.wait_ge(s_xt, PAIRS * p + b + 1)
                    act.activation(xh[:, :, 2 * P * b:2 * P * (b + 1)],
                                   bank[b].rearrange("p (c n) -> p c n", c=HC), ACT.Copy).then_inc(s_xh, 1)

            def inv_std_pair(b):
                inv_std(4 + b, pair_tiles(b))

            def highs_pair(b):
                act.wait_ge(s_xt, 2 * PAIRS + b + 1)
                act.activation(xh[:, :, 2 * P * b:2 * P * (b + 1)], turn_bank(b).rearrange("p (c n) -> p c n", c=HC),
                               ACT.Copy).then_inc(s_xh, 1)

            def high_gate_up(b, r, last):
                if last is not None:
                    act.wait_ge(s_u, last + 1)
                act.activation(wh[:, r, 0:GU], block_cols(b, 0, GU), ACT.Copy).then_inc(s_guh, 1)

            def high_down(b, r, last):
                if last is not None:
                    act.wait_ge(s_down, last + 1)
                act.activation(wh[:, r, GU:WB], block_cols(b, GU, WB), ACT.Copy).then_inc(s_dwh, 1)

            def half_step(f, j, k, first=False, last=False):
                s = STEPS * f + 4 * j + k
                act.wait_ge(s_g, s + 1)
                if not first:
                    act.wait_ge(s_hl, s - 3)
                act.activation(act_h[:, k, :], bank[4 + 2 * (k % 2)], ACT.Silu).then_inc(s_silu, 1)
                if first:
                    if k == 2:
                        high_gate_up(2, 0, s)
                elif last:
                    if k == 0:
                        high_gate_up(LAST + 1, 1, s - 1)
                elif k % 2 == 0:
                    high_gate_up(2 * j + k // 2 + 1, (k // 2 + 1) % 2, s - 1)
                if last and k == 3 and f == 0:
                    act.preload_act_table_set("natural_log_exp_and_others")
                act.wait_ge(s_h, s + 1)
                if not first:
                    act.wait_ge(s_down, s - 3)
                act.activation(hh[:, k, :], act_h[:, k, :], ACT.Copy).then_inc(s_hh, 1)
                if last:
                    if k < 2:
                        high_down(LAST + k, k, s - 2)
                elif k % 2 == 0 and not first:
                    high_down(2 * j + k // 2, k // 2, s - 2)

            def first_blocks(f, b):
                if f == 0:
                    act.wait_ge(s_w[b], 16)
                high_gate_up(b, b, STEPS * f - 2 + b if f else None)
                high_down(b, b, STEPS * f - 2 + b if f else None)

            def ffn(f):
                def split_small(k):
                    if f == 0:
                        act.activation(ah[:, small_part(k)], wsm[:, small_part(k)], ACT.Copy).then_inc(s_ah, 1)

                half_step(f, 0, 0, first=True)
                if f == 0:
                    act.wait_ge(s_small, 16)
                split_small(0)
                half_step(f, 0, 1, first=True)
                for h in range(2):
                    act.wait_ge(s_lp, 2 * f + h + 1)
                    act.activation(lgt[:, HALF * h:HALF * (h + 1)], bank[2 + h][0:2 * E, :], ACT.Copy).then_inc(s_lc, 1)
                split_small(1)
                act.wait_ge(s_logit, f + 1)
                act.activation(r8[:, 0, :], r8[:, 1, :], ACT.Exp, scale=-1.0).then_inc(s_er, 1)
                if f == 0:
                    act.wait_ge(s_w[2], 16 * 4)
                half_step(f, 0, 2, first=True)
                half_step(f, 0, 3, first=True)
                split_small(2)
                if f == 0:
                    act.activation(wv[:, :, 0, :], wsm[:, C_WV:C_RW].rearrange("p (c n) -> p c n", c=HC), ACT.Copy).then_inc(s_ah, 1)
                half_step(f, 1, 0)
                act.wait_ge(s_cwt, f + 1)
                act.activation(cwt[:], bank[4][0:TT * E, 0:P], ACT.Copy).then_inc(s_cwc, 1)
                for k in range(1, 4):
                    half_step(f, 1, k)
                with act.Fori(2, LAST // 2) as j:
                    for k in range(4):
                        half_step(f, j, k)
                for k in range(4):
                    half_step(f, LAST // 2, k, last=True)

            act.preload_act_table_set("natural_log_exp_and_others")
            for h in range(2):
                inv_std(h, half_tiles(h))
                first_blocks(0, h)
                if h:
                    act.preload_act_table_set("silu_and_others")
                highs(0, h)
            act.wait_ge(s_router, 16)
            act.wait_ge(s_rz, 1)
            act.activation(rw[:, :, 0:E], wsm[:, C_RW:C_END].rearrange("p (c e) -> p c e", c=HC), ACT.Copy).then_inc(s_rh, 1)
            ffn(0)
            inv_std(2, half_tiles(0))
            for h in range(2):
                a, z = h * TT // 2, (h + 1) * TT // 2
                if h == 0:
                    highs(1, 0)
                    inv_std(3, half_tiles(1))
                act.wait_ge(s_kp, h + 1)
                act.activation(kh[:, HALF * h:HALF * (h + 1)], bank[4], ACT.Copy).then_inc(s_kh, 1)
                for g in range(QG):
                    n = QG * h + g
                    act.wait_ge(s_qp, n + 1)
                    if n >= 2:
                        act.wait_ge(s_qs, n - 1)
                    act.activation(qh[:, n % 2, :], bank[5 + g % 2], ACT.Copy, scale=QK_SCALE).then_inc(s_qh, 1)
                    if True:
                        act.activation(qb[:, g % 2, :], bank[5 + g % 2], ACT.Copy, scale=kinds[:, 0:1]).then_inc(s_qb, 1)
                    if n == 1:
                        highs(1, 1)
                    if g == 1:
                        act.wait_ge(s_v, h + 1)
                        act.activation(vc[:, a + 1:z + 1, :, 0:D], vf[:, a + 1:z + 1, :, :], ACT.Copy).then_inc(s_vch, 1)
                    if g == 2:
                        act.wait_ge(s_vd, h + 1)
                        act.activation(vdc[:, a:z, :, 0:D], vd[:, a:z], ACT.Copy).then_inc(s_vch, 1)
            def unit(j, k, first=False, pair=None):
                u = 8 * j + k
                s = k % 2
                if not (first and k == 0):
                    probs_high(u - 1, 1 - s, first and k < 3)
                if pair is not None:
                    highs_pair(pair)
                if k in (1, 5) and not (first and k == 1):
                    inverse_sums(2 * j + (-1 if k == 1 else 0))
                if not (first and k < 2):
                    act.wait_ge(s_pt[1], u - 1)
                if k % 4 == 0 and not first:
                    act.wait_ge(s_rexp, 2 * j + k // 4 - 1)
                for h in range(QG):
                    lo = (h % 2) * 2 * P
                    if h % 2 == 0:
                        act.wait_ge(s_nm, 2 * u + h // 2 + 1)
                    i = act.activation(prob[:, s, h * P:(h + 1) * P], bank[2 * s + h // 2][:, lo:lo + P],
                                       ACT.Exp, bias=nmax[:, s, h:h + 1], accum_out=psums[:, k // 4, k % 4, h:h + 1])
                    if h % 2:
                        i.then_inc(s_exp[h // 2], 1)
                if k in (2, 6) and not (first and k == 2):
                    heads_high(2 * j + (-1 if k == 2 else 0))

            def probs_high(u, s, first):
                for b in range(2):
                    act.wait_ge(s_pt[b], u + 1)
                    if not first and b == 0:
                        act.wait_ge(s_av, u - 1)
                    act.activation(pall[:, s, 0, 2 * P * b:2 * P * (b + 1)], bank[4 + 3 * b][:, 0:2 * P], ACT.Copy)\
                       .then_inc(s_pah[b], 1)

            def inverse_sums(i, at=bank[5]):
                act.wait_ge(s_rt, i + 1)
                if not (isinstance(i, int) and i == 0):
                    act.wait_ge(s_att, i)
                act.activation(rden[:], at, ACT.Copy).then_inc(s_rden, 1)

            def heads_high(i):
                act.wait_ge(s_att, i + 1)
                if not (isinstance(i, int) and i == 0):
                    act.wait_ge(s_wo, i)
                act.activation(oh[:], att[:], ACT.Copy).then_inc(s_oh, 1)

            for b in range(2):
                first_blocks(1, b)
            for k in range(8):
                if k == 1:
                    act.wait_ge(s_qs, 2 * QG)
                unit(0, k, True)
            with act.Fori(1, LASTJ) as j:
                for k in range(8):
                    unit(j, k)
            for k in range(8):
                unit(LASTJ, k, pair={3: 0, 7: 1}.get(k))
                if k in (0, 3, 7):
                    inv_std_pair((k + 1) // 3)
            probs_high(UNITS - 1, 1, False)
            inverse_sums(TT - 1, bank[2])
            highs_pair(2)
            heads_high(TT - 1)
            inv_std_pair(3)
            act.preload_act_table_set("silu_and_others")
            highs_pair(3)
            ffn(1)

        @block.tensor
        def _(pe):
            def prep(p, h):
                if p == 0:
                    pe.wait_ge(s_pool, 6)
                for b in (2 * h, 2 * h + 1):
                    pe.wait_ge(s_xn, PAIRS * p + b + 1)
                    for c in range(HC):
                        for t in range(2):
                            at = (2 * c + t) * P
                            i = pe.transpose(bank[b][:, at:at + P], xn[:, 2 * b + t, c * P:(c + 1) * P], ident[:])
                    i.then_inc(s_xt, 1)

            def turn_pair(b):
                pe.wait_ge(s_xn, 2 * PAIRS + b + 1)
                for c in range(HC):
                    for t in range(2):
                        at = (2 * c + t) * P
                        i = pe.transpose(turn_bank(b)[:, at:at + P], xn2[:, b % 2, t, c * P:(c + 1) * P], ident[:])
                i.then_inc(s_xt, 1)

            def product(dst, left, right, n_left=None, first=True):
                pairs = [(0, 0), (0, 1), (1, 0)]
                chunks = len(left[0])
                for c in range(chunks):
                    for n, (a, b) in enumerate(pairs):
                        i = pe.matmul(dst, left[a][c], right[b][c], start=first and c == 0 and n == 0,
                                      stop=c == chunks - 1 and n == 2, skip_group_check=not first)
                return i

            def cols(w, at, n):
                return [w[:, at + c * n:at + (c + 1) * n] for c in range(HC)]

            def gate_up(f, j, k, t, r, first=False):
                s = STEPS * f + 4 * j + k
                if first:
                    pe.wait_ge(s_xl, PAIRS * 2 * f + 2 * t + 2)
                pe.wait_ge(s_gul, BLOCKS * f + 2 * j + r + 1)
                if not (first and k < 2):
                    pe.wait_ge(s_h, s - 1)
                for n, sm in ((0, s_g), (1, s_u)):
                    left = [[w[:, r, (2 * n + c) * P:(2 * n + c + 1) * P] for c in range(HC)] for w in (wh, wl)]
                    right = [[v[:, c, HALF * t:HALF * (t + 1)] for c in range(HC)] for v in (xh, xl)]
                    product(bank[4 + 2 * (k % 2) + n], left, right).then_inc(sm, 1)

            def down(f, j, k, t, r):
                pe.wait_ge(s_dwl, BLOCKS * f + 2 * j + r + 1)
                pe.wait_ge(s_hl, STEPS * f + 4 * j + k + 1)
                for tt in range(4):
                    tile_ = 4 * t + tt
                    dst = bank[tile_ // 2][:, (tile_ % 2) * H:(tile_ % 2 + 1) * H]
                    left = [[v[:, k, tt * P:(tt + 1) * P]] for v in (hh, hl)]
                    right = [[w[:, r, GU:WB]] for w in (wh, wl)]
                    i = product(dst, left, right, first=False)
                i.then_inc(s_down, 1)

            def open_sums(banks):
                for b in banks:
                    pe.matmul(bank[b], zeros[:, 0:P], zeros[:], start=True, stop=False, skip_group_check=True)

            def logits(h):
                n = 0
                for c in range(HC):
                    for v in (xh, xl):
                        i = pe.matmul(bank[2 + h], rw[:, c, :], v[:, c, HALF * h:HALF * (h + 1)],
                                      start=n == 0, stop=n == 2 * HC - 1)
                        n += 1
                i.then_inc(s_lp, 1)

            def turn_logits(f):
                pe.wait_ge(s_lc, 2 * f + 2)
                for t in range(TT):
                    i = pe.transpose(bank[2][:, t * 2 * E:(t + 1) * 2 * E], lgt[:, t * P:(t + 1) * P], ident[0:2 * E, 0:2 * E])
                i.then_inc(s_lt, 1)

            def ffn(f):
                if f == 0:
                    pe.wait_ge(s_rl, 1)
                    pe.wait_ge(s_xl, PAIRS)
                    for h in range(2):
                        logits(h)
                open_sums((0, 1))
                gate_up(f, 0, 2, 1, 0, True)
                turn_logits(f)
                down(f, 0, 0, 0, 0)
                down(f, 0, 1, 0, 1)
                gate_up(f, 0, 3, 1, 1, True)
                pe.wait_ge(s_logit, f + 1)
                open_sums((2, 3))
                gate_up(f, 1, 0, 0, 0)
                down(f, 0, 2, 1, 0)
                gate_up(f, 1, 1, 1, 0)
                down(f, 0, 3, 1, 1)
                pe.wait_ge(s_h, STEPS * f + 5)
                pe.wait_ge(s_cw, f + 1)
                pe.transpose(bank[4][0:TT * E, 0:P], r8[:, 6, :], ident[:]).then_inc(s_cwt, 1)
                pe.wait_ge(s_cwc, f + 1)

                def rest_of_pair(j):
                    gate_up(f, j, 2, 0, 1)
                    down(f, j, 0, 0, 0)
                    gate_up(f, j, 3, 1, 1)
                    down(f, j, 1, 1, 0)

                with pe.Fori(1, LAST // 2 - 1) as j:
                    rest_of_pair(j)
                    gate_up(f, j + 1, 0, 0, 0)
                    down(f, j, 2, 0, 1)
                    gate_up(f, j + 1, 1, 1, 0)
                    down(f, j, 3, 1, 1)
                z = LAST // 2
                rest_of_pair(z - 1)
                gate_up(f, z, 0, 0, 0)
                down(f, z - 1, 2, 0, 1)
                gate_up(f, z, 1, 0, 1)
                down(f, z - 1, 3, 1, 1)
                gate_up(f, z, 2, 1, 0)
                down(f, z, 0, 0, 0)
                if f == 0:
                    down(f, z, 1, 0, 1)
                gate_up(f, z, 3, 1, 1)
                if f == 1:
                    down(f, z, 1, 0, 1)
                down(f, z, 2, 1, 0)
                down(f, z, 3, 1, 1)

            parts = lambda at, n: [cols(w, at, n) for w in (ah, al)]
            xs = lambda a, z: [[v[:, c, a:z] for c in range(HC)] for v in (xh, xl)]

            pe.wait_ge(s_zeros, 1)
            for n in range(WARM):
                pe.matmul(bank[7], zeros[:, 0:P], zeros[:], start=True, stop=True)
            prep(0, 0)
            gate_up(0, 0, 0, 0, 0, True)
            prep(0, 1)
            gate_up(0, 0, 1, 0, 1, True)
            ffn(0)
            prep(1, 0)
            for h in range(2):
                pe.wait_ge(s_xl, PAIRS + 2 * h + 2)
                if h:
                    pe.wait_ge(s_kl, h)
                product(bank[4], parts(C_WK, P), xs(HALF * h, HALF * (h + 1))).then_inc(s_kp, 1)
                if h:
                    pe.wait_ge(s_v, h)
                for t in range(TT // 2):
                    at = HALF * h + t * P
                    n = 0
                    for c in range(HC):
                        for v in (xh, xl):
                            i = pe.matmul(bank[7][:, t * P:(t + 1) * P], v[:, c, at:at + P],
                                          wv[:, c, :, :].rearrange("p a n -> p (a n)"), start=n == 0, stop=n == 2 * HC - 1)
                            n += 1
                i.then_inc(s_vp, 1)
                for g in range(QG):
                    n = QG * h + g
                    if n >= 2:
                        pe.wait_ge(s_qb, n - 1)
                    left = [[w[:, C_WQ + (c * QG + g) * P:C_WQ + (c * QG + g + 1) * P] for c in range(HC)] for w in (ah, al)]
                    product(bank[5 + g % 2], left, xs(HALF * h, HALF * (h + 1))).then_inc(s_qp, 1)
                    if n == 1:
                        prep(1, 1)

            def scores(j, k, first):
                u, s, g, r = 8 * j + k, k % 2, k % 4, k // 4
                if g == 0:
                    pe.wait_ge(s_tkeys[r], 16 * (j + 1))
                if g % 2 == 0:
                    pe.wait_ge(s_queries[r][g // 2], 4 * 16 * (j + 1))
                if not (first and k < 2):
                    pe.wait_ge(s_exp[1], u - 1)
                rows = slice(2 * GR * (g % 2), 2 * GR * (g % 2 + 1))
                for h in range(QG):
                    q = qring[rows, r, g // 2, h * P:(h + 1) * P]
                    lo = (h % 2) * 2 * P
                    b = bank[2 * s + h // 2]
                    if first and r == 0:
                        pe.matmul(b[:, lo:lo + P], negs[rows, 0:P], negs[rows, P:2 * P], start=True, stop=True)
                        i = pe.matmul(b[:, lo + P:lo + 2 * P], q, kring[rows, r, g // 2, P:2 * P], start=True, stop=True)
                    else:
                        i = pe.matmul(b[:, lo:lo + 2 * P], q, kring[rows, r, g // 2, :], start=True, stop=True)
                    if h % 2:
                        i.then_inc(s_qk[h // 2], 1)

            def turn(u, s, first=False):
                for b in range(2):
                    pe.wait_ge(s_exp[b], u + 1)
                    if not first:
                        pe.wait_ge(s_pal[b], u)
                    for h in range(2):
                        at = (2 * b + h) * P
                        i = pe.transpose(bank[4 + 3 * b][:, h * P:(h + 1) * P], prob[:, s, at:at + P], ident[:])
                    i.then_inc(s_pt[b], 1)

            def values(j, g, s, r, first=False):
                i = 2 * j + r
                pe.wait_ge(s_pal[1], 4 * i + g + 1)
                if g == 0:
                    pe.wait_ge(s_vr[r], 32 * (j + 1))
                    if not first:
                        pe.wait_ge(s_att, i)
                cs = slice(g * P, (g + 1) * P)
                for w in range(2):
                    o = g == 0 and w == 0
                    pe.matmul(bank[6], vprev[:, r, cs], pall[:, s, w, :], start=o, stop=False, skip_group_check=True)
                for w in range(2):
                    pe.wait_ge(s_pm, 8 * i + 2 * g + w + 1)
                    m = pe.matmul(bank[6], vdiff[:, r, cs], pcur[:, s, w, :], start=False, stop=g == KV - 1 and w == 1, skip_group_check=True)
                m.then_inc(s_av, 1)

            def turn_sums(i, at=bank[5]):
                pe.wait_ge(s_rexp, i + 1)
                for h in range(QG):
                    m = pe.transpose(at[:, h * P:(h + 1) * P], rexp[:, h, :, :].rearrange("p g r -> p (g r)"), ident[:])
                m.then_inc(s_rt, 1)

            def project(i, at=bank[5]):
                pe.wait_ge(s_ol, i + 1)
                if at is bank[5] and not (isinstance(i, int) and i == TT - 2):
                    pe.wait_ge(s_rden, i + 2)
                left = [[v[:, h * P:(h + 1) * P] for h in range(QG)] for v in (oh, ol)]
                right = [[w[:, C_WO + h * H:C_WO + (h + 1) * H] for h in range(QG)] for w in (ah, al)]
                product(at[:, 0:H], left, right).then_inc(s_wo, 1)

            def step(j, k, first=False, pair_0=False):
                scores(j, k, first)
                if pair_0:
                    pe.wait_ge(s_xl, 2 * PAIRS + 1)
                if k in (1, 5) and not (first and k == 1):
                    turn_sums(2 * j + (0 if k == 5 else -1))
                if not (first and k == 0):
                    turn(8 * j + k - 1, (k + 1) % 2, first and k == 1)
                if not (first and k < 2):
                    values(j + (k - 2) // 8, (k - 2) % 4, k % 2, ((k - 2) // 4) % 2, first and k < 6)
                if k in (1, 5) and not first:
                    project(2 * j + (-1 if k == 5 else -2))

            for k in range(8):
                if k == 1:
                    pe.wait_ge(s_kl, 2)
                    pe.wait_ge(s_qb, 2 * QG)
                step(0, k, True)
            with pe.Fori(1, LASTJ) as j:
                for k in range(8):
                    step(j, k)
            for k in range(8):
                step(LASTJ, k, pair_0=k == 5)
                if k in (2, 6):
                    pe.wait_ge(s_x2, TT - 3 + k // 4)
                    turn_pair(k // 4)
            turn(UNITS - 1, 1)
            values(LASTJ, 2, 0, 1)
            turn_sums(TT - 1, bank[2])
            pe.wait_ge(s_xl, 2 * PAIRS + 2)
            project(TT - 2)
            turn_pair(2)
            values(LASTJ, 3, 1, 1)
            pe.wait_ge(s_pal[0], UNITS)
            pe.wait_ge(s_x2, TT - 1)
            gate_up(1, 0, 0, 0, 0, True)
            project(TT - 1, bank[3])
            pe.wait_ge(s_att, TT)
            pe.wait_ge(s_pal[1], UNITS)
            gate_up(1, 0, 1, 0, 1, True)
            logits(0)
            turn_pair(3)
            pe.wait_ge(s_xl, 3 * PAIRS)
            pe.wait_ge(s_x2, TT)
            logits(1)
            ffn(1)

        @block.vector
        def _(dve):
            links = [0]

            def link(i):
                links[0] += 1
                i.then_inc(s_dve, 1)
                dve.wait_ge(s_dve, links[0])

            def tiles(ts):
                return range(ts.start, ts.stop)

            def bn(ts):
                for t in tiles(ts):
                    i = dve.bn_stats(bst[:, t, :], x[:, t, :])
                link(i)

            def variance(ts):
                for t in tiles(ts):
                    i = dve.bn_aggr(mv[:, t, :], bst[:, t, :])
                link(i)
                dve.tensor_scalar(ve[:, ts], mv[:, ts, 1], EPS, None, ALU.add).then_inc(s_ve, 1)

            def norm(n, ts, to):
                dve.wait_ge(s_ln, 2 * n + 2)
                link(dve.scalar_tensor_tensor(out=nt[:, 0, ts], in0=ve[:, ts], scalar=-0.5, in1=rs[:, ts],
                                              op0=ALU.mult, op1=ALU.mult))
                link(dve.tensor_tensor(nt[:, 1, ts], nt[:, 0, ts], rs[:, ts], ALU.mult))
                link(dve.scalar_tensor_tensor(out=rs[:, ts], in0=nt[:, 1, ts], scalar=1.5, in1=rs[:, ts],
                                              op0=ALU.add, op1=ALU.mult))
                for t in tiles(ts):
                    i = dve.tensor_scalar(to(t), x[:, t, :], mv[:, t, 0:1], rs[:, t:t + 1], ALU.subtract, ALU.mult)
                    if t % 2:
                        i.then_inc(s_xn, 1)

            def norm_half(p, h):
                norm(2 * p + h, half_tiles(h), lambda t: xn[:, t, :])

            def bn_pair(b):
                dve.wait_ge(s_x2, 2 * b + 2)
                bn(pair_tiles(b))
                variance(pair_tiles(b))

            def norm_pair(b):
                norm(4 + b, pair_tiles(b), lambda t: xn2[:, b % 2, t % 2, :])

            def lows_pair(b):
                dve.wait_ge(s_xh, 2 * PAIRS + b + 1)
                cs = slice(2 * P * b, 2 * P * (b + 1))
                dve.tensor_tensor(xl[:, :, cs], turn_bank(b).rearrange("p (c n) -> p c n", c=HC),
                                  xh[:, :, cs].bitcast(F32), ALU.subtract).then_inc(s_xl, 1)

            def lows(p, h):
                for b in (2 * h, 2 * h + 1):
                    dve.wait_ge(s_xh, PAIRS * p + b + 1)
                    cs = slice(2 * P * b, 2 * P * (b + 1))
                    dve.tensor_tensor(xl[:, :, cs], bank[b].rearrange("p (c n) -> p c n", c=HC),
                                      xh[:, :, cs].bitcast(F32), ALU.subtract).then_inc(s_xl, 1)

            def route_scores(f):
                dve.wait_ge(s_lt, f + 1)
                lg = bank[2][:, 0:2 * TT * E].rearrange("p (t a e) -> p t a e", a=2, e=E)
                link(dve.tensor_copy(v3(r8[:, 0, :], E), lg[:, :, 0, :]))
                dve.tensor_tensor(v3(r8[:, 1, :], E), lg[:, :, 1, :], v3(r8[:, 0, :], E), ALU.add).then_inc(s_logit, 1)

            def compare(vals, n, above, equal):
                a = vals.unsqueeze(3).to_broadcast([P, TT, n, n])
                b = vals.unsqueeze(2).to_broadcast([P, TT, n, n])
                v4 = lambda ap: ap.rearrange("p (t i j) -> p t i j", i=n, j=n)
                dve.tensor_tensor(v4(above), b, a, ALU.is_gt)
                link(dve.tensor_tensor(v4(equal), b, a, ALU.is_equal))

            def count(n, tie, above, equal, dst):
                q = equal.rearrange("p (t m) -> p t m", t=TT)
                link(dve.tensor_tensor(q, q, tie[:].rearrange("p i j -> p (i j)").unsqueeze(1).to_broadcast([P, TT, n * n]), ALU.mult))
                link(dve.tensor_tensor(above, above, equal, ALU.add))
                link(dve.tensor_reduce(dst, above.rearrange("p (m j) -> p m j", j=n), AX_X, ALU.add))

            v3 = lambda ap, n: ap.rearrange("p (t e) -> p t e", e=n)
            pairs = r8[:, 3, :].rearrange("p (g two) -> p g two", two=2)

            def route_groups(f):
                dve.wait_ge(s_er, f + 1)
                link(dve.tensor_scalar(r8[:, 1, :], r8[:, 0, :], 1.0, None, ALU.add))
                link(dve.reciprocal(r8[:, 2, :], r8[:, 1, :]))
                if f == 0:
                    dve.wait_ge(s_const, 48)
                    dve.wait_ge(s_pool, 6)
                sfc = v3(r8[:, 3, :], E)
                link(dve.tensor_tensor(sfc, v3(r8[:, 2, :], E), rbias[:].unsqueeze(1).to_broadcast([P, TT, E]), ALU.add))
                link(dve.tensor_tensor(r4[:, 0, :], pairs[:, :, 0], pairs[:, :, 1], ALU.add))

                compare(v3(r4[:, 0, :], NG), NG, r16[:, 0, :], r16[:, 1, :])
                count(NG, tie4, r16[:, 0, :], r16[:, 1, :], r4[:, 1, :])
                link(dve.tensor_scalar(r4[:, 2, :], r4[:, 1, :], 2.0, None, ALU.is_lt))
                gm = r4[:, 2, :].unsqueeze(2).to_broadcast([P, TT * NG, 2])
                link(dve.tensor_tensor(r8[:, 4, :].rearrange("p (g two) -> p g two", two=2), pairs, gm, ALU.mult))

            def route_experts(f):
                big = cwb[:, 3, :].rearrange("p (a n) -> p a n", a=2)
                compare(v3(r8[:, 4, :], E), E, big[:, 0, :], big[:, 1, :])
                hidden(f, 0, 3)
                count(E, tie8, big[:, 0, :], big[:, 1, :], r8[:, 5, :])

            def route_weights(f):
                link(dve.tensor_scalar(r8[:, 5, :], r8[:, 5, :], 2.0, None, ALU.is_lt))
                link(dve.tensor_tensor(r8[:, 5, :], r8[:, 5, :], r8[:, 2, :], ALU.mult))
                link(dve.tensor_reduce(r4[:, 3, 0:TT], v3(r8[:, 5, :], E), AX_X, ALU.add))
                link(dve.tensor_scalar(r4[:, 3, 0:TT], r4[:, 3, 0:TT], 1e-20, None, ALU.add))
                link(dve.reciprocal(r4[:, 3, TT:2 * TT], r4[:, 3, 0:TT]))
                link(dve.tensor_scalar(r4[:, 3, TT:2 * TT], r4[:, 3, TT:2 * TT], SCALE, None, ALU.mult))
                cw = r8[:, 6, :].rearrange("p (e t) -> p t e", e=E)
                dve.tensor_tensor(cw, v3(r8[:, 5, :], E), r4[:, 3, TT:2 * TT].unsqueeze(2).to_broadcast([P, TT, E]),
                                  ALU.mult).then_inc(s_cw, 1)


            def hidden(f, j, k, row=None):
                s = STEPS * f + 4 * j + k
                h = act_h[:, k, :]
                dve.wait_ge(s_silu, s + 1)
                if row is not None:
                    n = s + 1 - 2 * SH_BLOCKS * (f + 1)
                    dve.tensor_tensor(h, h, row, ALU.mult).then_inc(s_cwm, 1)
                    dve.wait_ge(s_cwm, n)
                dve.wait_ge(s_u, s + 1)
                dve.tensor_tensor(h, bank[5 + 2 * (k % 2)], h, ALU.mult).then_inc(s_h, 1)

            def hidden_low(f, j, k):
                dve.wait_ge(s_hh, STEPS * f + 4 * j + k + 1)
                dve.tensor_tensor(hl[:, k, :], act_h[:, k, :], hh[:, k, :].bitcast(F32), ALU.subtract).then_inc(s_hl, 1)

            def half_step(f, j, k, row=None):
                hidden(f, j, k, row)
                hidden_low(f, j, k)

            def finish(f, h):
                dve.wait_ge(s_down, STEPS * (f + 1) - 2 + 2 * h)
                for b in (2 * h, 2 * h + 1):
                    xs = x[:, 2 * b:2 * b + 2, :].rearrange("p t h -> p (t h)")
                    i = dve.scalar_tensor_tensor(out=xs, in0=bank[b], scalar=0.5, in1=xs, op0=ALU.mult, op1=ALU.add)
                    i.then_inc(s_fin, 1)

            def ffn(f):
                def row_of(b, t):
                    if isinstance(b, int):
                        return cwb[:, b - SH_BLOCKS, HALF * t:HALF * (t + 1)]
                    return cwb[:, bass.ds(b - SH_BLOCKS, 1), HALF * t:HALF * (t + 1)].rearrange("p a n -> p (a n)")

                def pair(j):
                    for k in range(4):
                        half_step(f, j, k, row_of(2 * j + k // 2, k % 2))

                half_step(f, 0, 0)
                half_step(f, 0, 1)
                route_scores(f)
                route_groups(f)
                half_step(f, 0, 2)
                route_experts(f)
                hidden(f, 1, 0)
                hidden_low(f, 0, 3)
                route_weights(f)
                hidden_low(f, 1, 0)
                half_step(f, 1, 1)
                dve.wait_ge(s_cwb[0], 16 * N_CWB[0] * (f + 1))
                half_step(f, 1, 2, row_of(3, 0))
                half_step(f, 1, 3, row_of(3, 1))
                dve.wait_ge(s_cwb[1], 16 * N_CWB[1] * (f + 1))
                with dve.Fori(2, 4) as j:
                    pair(j)
                dve.wait_ge(s_cwb[2], 16 * N_CWB[2] * (f + 1))
                with dve.Fori(4, LAST // 2) as j:
                    pair(j)
                z = LAST // 2
                half_step(f, z, 0, row_of(LAST, 0))
                half_step(f, z, 1, row_of(LAST + 1, 0))
                half_step(f, z, 2, row_of(LAST, 1))
                if f == 0:
                    finish(f, 0)
                    dve.wait_ge(s_fin, 2)
                    bn(half_tiles(0))
                hidden(f, z, 3, row_of(LAST + 1, 1))
                if f == 0:
                    variance(half_tiles(0))
                hidden_low(f, z, 3)
                if f == 0:
                    norm_half(1, 0)
                    lows(1, 0)
                else:
                    finish(f, 0)
                finish(f, 1)

            dve.wait_ge(s_x[0], 16)
            bn(half_tiles(0))
            variance(half_tiles(0))
            norm_half(0, 0)
            dve.wait_ge(s_x[1], 16)
            bn(half_tiles(1))
            lows(0, 0)
            variance(half_tiles(1))
            norm_half(0, 1)
            lows(0, 1)
            ffn(0)

            def pick_max(j, k):
                u, s = 8 * j + k, k % 2
                for b in range(2):
                    v = bank[2 * s + b].rearrange("p (h w k) -> p h w k", h=2, w=2)
                    dve.wait_ge(s_qk[b], u + 1)
                    dve.memset(idle[:, 2 * s + b:2 * s + b + 1], 0.0)
                    dve.copy_predicated(v[:, :, 0, :], sel_q[:].bitcast(I32), v[:, :, 1, :]).then_inc(s_sel, 1)
                for b in range(2):
                    v = bank[2 * s + b].rearrange("p (h w k) -> p h w k", h=2, w=2)
                    dve.wait_ge(s_sel, 2 * u + b + 1)
                    dve.tensor_reduce(nmax[:, s, 2 * b:2 * b + 2], v[:, :, 0, :], AX_X, ALU.max, negate=True).then_inc(s_nm, 1)

            def keys_low(h):
                cs = slice(HALF * h, HALF * (h + 1))
                dve.wait_ge(s_kh, h + 1)
                dve.tensor_tensor(kl[:, cs], bank[4], kh[:, cs].bitcast(F32), ALU.subtract).then_inc(s_kl, 1)

            def take_values(h):
                dve.wait_ge(s_vp, h + 1)
                v = bank[7].rearrange("p (t a g d) -> p t a g d", a=2, g=KV, d=D)
                to = vf[:, 1 + h * TT // 2:1 + (h + 1) * TT // 2, :, :]
                link(dve.tensor_copy(to, v[:, :, 0, :, :]))
                dve.tensor_tensor(to, v[:, :, 1, :, :], to, ALU.add).then_inc(s_v, 1)

            def both_parts(h):
                for g in range(QG):
                    n = QG * h + g
                    if n == 2 * QG - 1:
                        pick_max(0, 0)
                    dve.wait_ge(s_qh, n + 1)
                    dve.wait_ge(s_qb, n + 1)
                    dve.scalar_tensor_tensor(out=qs[:, g, HALF * h:HALF * (h + 1)],
                                             in0=qh[:, n % 2, :].bitcast(F32), scalar=kinds[:, 1:2], in1=qb[:, n % 2, :],
                                             op0=ALU.mult, op1=ALU.add).then_inc(s_qs, 1)
                    if n == 1:
                        lows(1, 1)

            dve.wait_ge(s_fin, PAIRS)
            dve.wait_ge(s_pads, 2)
            bn(half_tiles(1))
            variance(half_tiles(1))
            keys_low(0)
            norm_half(1, 1)
            take_values(0)
            both_parts(0)
            keys_low(1)
            take_values(1)
            both_parts(1)

            def probs_low(u, s):
                for b in range(2):
                    cs = slice(2 * P * b, 2 * P * (b + 1))
                    dve.wait_ge(s_pah[b], u + 1)
                    dve.tensor_tensor(pall[:, s, 1, cs], bank[4 + 3 * b][:, 0:2 * P], pall[:, s, 0, cs].bitcast(F32),
                                      ALU.subtract).then_inc(s_pal[b], 1)

            def invert_sums(i, k):
                dve.wait_ge(s_exp[1], 4 * i + 4)
                dve.reciprocal(rsums[:], psums[:, k, :, :]).then_inc(s_rd, 1)
                if not (isinstance(i, int) and i == 0):
                    dve.wait_ge(s_rt, i)
                dve.wait_ge(s_rd, i + 1)
                dve.tensor_copy(rexp[:], rsums[:].rearrange("p g h -> p h g").unsqueeze(3).to_broadcast([P, QG, KV, GR]))\
                   .then_inc(s_rexp, 1)

            def normalise(i):
                dve.wait_ge(s_av, 4 * i + 4)
                if not (isinstance(i, int) and i == 0):
                    dve.wait_ge(s_ol, i)
                dve.wait_ge(s_rden, i + 1)
                dve.tensor_tensor(att[:], bank[6], rden[:], ALU.mult).then_inc(s_att, 1)

            def add_heads(i, at=bank[5]):
                dve.wait_ge(s_wo, i + 1)
                xs = x[:, i, :] if isinstance(i, int) else x[:, bass.ds(i, 1), :].rearrange("p a n -> p (a n)")
                dve.tensor_tensor(xs, at[:, 0:H], xs, ALU.add).then_inc(s_x2, 1)

            def step(j, k, first=False, pair=None):
                if not (first and k == 0):
                    pick_max(j, k)
                if k == 4:
                    invert_sums(2 * j, 0)
                if k == 0 and not first:
                    invert_sums(2 * j - 1, 1)
                if not (first and k == 0):
                    probs_low(8 * j + k - 1, (k + 1) % 2)
                if pair is not None:
                    lows_pair(pair)
                if k == 5:
                    normalise(2 * j)
                if k == 1 and not first:
                    normalise(2 * j - 1)
                if k in (2, 6) and not first:
                    add_heads(2 * j + (-1 if k == 6 else -2))

            for k in range(8):
                step(0, k, True)
            dve.wait_ge(s_xb, TT)
            with dve.Fori(1, LASTJ) as j:
                for k in range(8):
                    step(j, k)
            bn_pair(0)
            for k in range(8):
                step(LASTJ, k, pair=0 if k == 4 else None)
                if k in (2, 6):
                    bn_pair((k + 2) // 4)
                if k in (1, 4):
                    norm_pair(k // 3)
            lows_pair(1)
            invert_sums(TT - 1, 1)
            probs_low(UNITS - 1, 1)
            norm_pair(2)
            add_heads(TT - 2)
            lows_pair(2)
            normalise(TT - 1)
            dve.wait_ge(s_oh, TT)
            dve.wait_ge(s_wo, TT - 1)
            dve.tensor_tensor(ol[:], att[:], oh[:].bitcast(F32), ALU.subtract).then_inc(s_ol, 1)
            add_heads(TT - 1, bank[3])
            bn_pair(3)
            norm_pair(3)
            lows_pair(3)
            ffn(1)


def _lay_out(np, a):
    def hidden_rows(shared, routed):
        pad = np.zeros((SH_BLOCKS * P - I_SHARED, H), np.float32)
        rows = np.concatenate([shared, pad, routed.reshape(E * I_MOE, H)])
        return rows.reshape(BLOCKS, P, H)

    gate = hidden_rows(a["L0_ffn_shared_gate_w"], a["L0_ffn_gate_w"]).reshape(BLOCKS, P, HC, P)
    up = hidden_rows(a["L0_ffn_shared_up_w"], a["L0_ffn_up_w"]).reshape(BLOCKS, P, HC, P)
    down = hidden_rows(a["L0_ffn_shared_down_w"].T, a["L0_ffn_down_w"].transpose(0, 2, 1))
    to_cols = lambda w: w.transpose(3, 0, 2, 1).reshape(P, BLOCKS, HC * P)
    blocks = np.concatenate([to_cols(gate), to_cols(up), down.transpose(1, 0, 2)], axis=2)

    wq = a["L0_attn_Wq"].reshape(HC, P, KV, QG, 1, D)
    wq = np.concatenate([wq, wq], axis=4).transpose(1, 0, 3, 2, 4, 5).reshape(P, HC * QG * P)
    wk = a["L0_attn_Wk"].reshape(HC, P, KV, 1, D)
    wk = np.concatenate([wk, wk], axis=3).transpose(1, 0, 2, 3, 4).reshape(P, HC * P)
    wv = a["L0_attn_Wv"].reshape(HC, P, KV * D).transpose(1, 0, 2).reshape(P, HC * KV * D)
    wo = a["L0_attn_Wo"].reshape(KV, QG, 1, D, H)
    wo = np.concatenate([wo, wo], axis=2).transpose(0, 2, 3, 1, 4).reshape(P, QG * H)
    rw = a["L0_ffn_router_weight"].T.reshape(HC, P, E).transpose(1, 0, 2).reshape(P, HC * E)
    small = np.concatenate([wq, wk, wo, wv, rw], axis=1)

    kinds = np.zeros((P // (2 * D), 2, D, 2), np.float32)
    kinds[:, 0, :, 1] = 1.0
    kinds[:, 1, :, 0] = QK_SCALE
    kinds[:, 1, :, 1] = -1.0
    return {
        "x_in": a["L0_attn_x"], "w_blocks": blocks, "w_small": small, "row_kind": kinds.reshape(P, 2),
        "router_bias": a["L0_ffn_e_score_correction_bias"], "out_bias": a["L0_attn_bo"],
    }


def kernel(**inputs):
    import numpy as np
    import concourse.bacc as bacc
    from concourse import mybir as _mybir
    from concourse.bass_utils import run_bass_kernel_spmd as run

    nc = bacc.Bacc("TRN2", target_bir_lowering=False, num_devices=1)
    arrays = {k: np.ascontiguousarray(v) for k, v in _lay_out(np, {k: np.asarray(v) for k, v in inputs.items()}).items()}
    args = [nc.dram_tensor(k, v.shape, _mybir.dt.from_np(v.dtype), kind="ExternalInput").ap() for k, v in arrays.items()]
    out = nc.dram_tensor("out_dram", (1, T, H), F32, kind="ExternalOutput").ap()
    macaron_kernel(nc, *args, out)
    return run(nc, [arrays], core_ids=[0]).results[0]["out_dram"]
```
